# Optimizing a Trainium2 kernel written in Bass

```python
import numpy as np
import jax
import jax.numpy as jnp

def _softmax(x, axis=-1):
    return jax.nn.softmax(x, axis=axis)

def _gelu(x):
    return jax.nn.gelu(x, approximate=True)

def _silu(x):
    return jax.nn.silu(x)

def _sigmoid(x):
    return jax.nn.sigmoid(x)

def _layernorm(x, axis=-1, eps=1e-05):
    m = jnp.mean(x, axis=axis, keepdims=True)
    v = jnp.var(x, axis=axis, keepdims=True)
    return (x - m) / jnp.sqrt(v + eps)

def _scatter_add(tgt, idx, src, axis=0):
    return tgt.at[idx].add(src)

def _segment_sum(src, seg, n):
    return jax.ops.segment_sum(src, seg, n)
kernel_name = 'mk_flamingo_gated_d1_seqx_r4_f09ae3'

def setup_inputs(seed: int=0):
    np.random.seed(seed)
    _w = jnp.asarray

    def _rec_inputs():
        import jax
        import jax.numpy as jnp
        _rk = jax.random.key(seed)
        x = 7.22e-05 + 1 * jax.random.normal(jax.random.fold_in(_rk, 1), (8, 256, 256), jnp.float32)
        _lenS = 256 - jax.random.randint(jax.random.fold_in(_rk, 7), (8,), 0, max(1, 256 // 4) + 1, jnp.int32)
        _lenS2 = 77 - jax.random.randint(jax.random.fold_in(_rk, 8), (8,), 0, max(1, 77 // 4) + 1, jnp.int32)
        _ctx_1024P = jax.random.normal(jax.random.fold_in(_rk, 11), (8, 16, 256), jnp.float32)
        _ctx_1024c = jax.random.dirichlet(jax.random.fold_in(_rk, 511), 0.3 * jnp.ones((16,), jnp.float32), (8, 77))
        _ctx_1024t = jnp.einsum('bsk,bkd->bsd', _ctx_1024c, _ctx_1024P)
        _ctx_1024t = _ctx_1024t * jax.lax.rsqrt(jnp.mean(jnp.square(_ctx_1024t)) + 1e-12) * 0.953939
        ctx_1024 = 4.13588e-05 + 0.999923 * (_ctx_1024t + 0.3 * jax.random.normal(jax.random.fold_in(_rk, 611), (8, 77, 256), jnp.float32))
        _validS = jnp.arange(256)[None, :] < _lenS[:, None]
        _validS2 = jnp.arange(77)[None, :] < _lenS2[:, None]
        _causal = jnp.tril(jnp.ones((256, 256), dtype=bool))
        mask_BxS2_bf0 = jnp.logical_not(jnp.ones((8, 77), dtype=bool))
        _g = jax.random.normal(jax.random.fold_in(_rk, 9001), (2, 1), jnp.float32)
        _g = jnp.sign(_g) * jnp.maximum(jnp.abs(_g), 1.0) + (_g == 0) * 1.0
        g_xattn = _g[0]
        g_ffn = _g[1]
        return (x, ctx_1024, mask_BxS2_bf0, g_xattn, g_ffn)
    x, ctx_1024, mask_BxS2_bf0, g_xattn, g_ffn = _rec_inputs()

    def _L0_xattn_setup():
        import jax, jax.numpy as jnp
        import numpy as np
        DIM = 256
        N_HEAD = 16
        BS, QLEN, KLEN = (4, 512, 512)
        key = jax.random.key(seed)
        ks = jax.random.split(key, 12)
        s = 1.0 / np.sqrt(DIM)
        inp = {'q_in': jax.random.normal(ks[0], (BS, QLEN, DIM), jnp.float32), 'k_in': jax.random.normal(ks[1], (BS, KLEN, DIM), jnp.float32), 'v_in': jax.random.normal(ks[2], (BS, KLEN, DIM), jnp.float32), 'key_padding_mask': jnp.zeros((BS, KLEN), dtype=bool), 'Wq': jax.random.normal(ks[3], (DIM, DIM), jnp.float32) * s, 'bq': jnp.zeros((DIM,), jnp.float32), 'Wk': jax.random.normal(ks[4], (DIM, DIM), jnp.float32) * s, 'bk': jnp.zeros((DIM,), jnp.float32), 'Wv': jax.random.normal(ks[5], (DIM, DIM), jnp.float32) * s, 'bv': jnp.zeros((DIM,), jnp.float32), 'Wo': jax.random.normal(ks[6], (DIM, DIM), jnp.float32) * s, 'bo': jnp.zeros((DIM,), jnp.float32)}
        return inp
    _L0_xattn_all = _L0_xattn_setup()
    _L0_xattn_in = {k: v for k, v in _L0_xattn_all.items() if k in ('Wq', 'bq', 'Wk', 'bk', 'Wv', 'bv', 'Wo', 'bo')}
    del _L0_xattn_all

    def _L0_ffn_setup():
        import jax, jax.numpy as jnp
        import numpy as np
        TOP_K = 2
        key = jax.random.key(seed)
        ks = jax.random.split(key, 6)
        B, S, H, F, E = (4, 512, 256, 1024, 8)
        x = jax.random.normal(ks[0], (B, S, H), dtype=jnp.float32)
        gate_w = jax.random.normal(ks[1], (E, H), dtype=jnp.float32) * 0.02
        W1 = jax.random.normal(ks[2], (E, H, F), dtype=jnp.float32) * (1.0 / np.sqrt(H))
        b1 = jnp.zeros((E, F), dtype=jnp.float32)
        W2 = jax.random.normal(ks[3], (E, F, H), dtype=jnp.float32) * (1.0 / np.sqrt(F))
        b2 = jnp.zeros((E, H), dtype=jnp.float32)
        sW1 = jax.random.normal(ks[4], (H, F), dtype=jnp.float32) * (1.0 / np.sqrt(H))
        sb1 = jnp.zeros((F,), dtype=jnp.float32)
        sW2 = jax.random.normal(ks[5], (F, H), dtype=jnp.float32) * (1.0 / np.sqrt(F))
        sb2 = jnp.zeros((H,), dtype=jnp.float32)
        return {'x': x, 'gate_w': gate_w, 'W1': W1, 'b1': b1, 'W2': W2, 'b2': b2, 'sW1': sW1, 'sb1': sb1, 'sW2': sW2, 'sb2': sb2}
    _L0_ffn_all = _L0_ffn_setup()
    _L0_ffn_in = {k: v for k, v in _L0_ffn_all.items() if k in ('gate_w', 'W1', 'b1', 'W2', 'b2', 'sW1', 'sb1', 'sW2', 'sb2')}
    del _L0_ffn_all
    return {'x': x, 'ctx_1024': ctx_1024, 'mask_BxS2_bf0': mask_BxS2_bf0, 'g_xattn': g_xattn, 'g_ffn': g_ffn, 'L0_xattn_Wq': _L0_xattn_in['Wq'], 'L0_xattn_bq': _L0_xattn_in['bq'], 'L0_xattn_Wk': _L0_xattn_in['Wk'], 'L0_xattn_bk': _L0_xattn_in['bk'], 'L0_xattn_Wv': _L0_xattn_in['Wv'], 'L0_xattn_bv': _L0_xattn_in['bv'], 'L0_xattn_Wo': _L0_xattn_in['Wo'], 'L0_xattn_bo': _L0_xattn_in['bo'], 'L0_ffn_gate_w': _L0_ffn_in['gate_w'], 'L0_ffn_W1': _L0_ffn_in['W1'], 'L0_ffn_b1': _L0_ffn_in['b1'], 'L0_ffn_W2': _L0_ffn_in['W2'], 'L0_ffn_b2': _L0_ffn_in['b2'], 'L0_ffn_sW1': _L0_ffn_in['sW1'], 'L0_ffn_sb1': _L0_ffn_in['sb1'], 'L0_ffn_sW2': _L0_ffn_in['sW2'], 'L0_ffn_sb2': _L0_ffn_in['sb2']}

def reference(x, ctx_1024, mask_BxS2_bf0, g_xattn, g_ffn, L0_xattn_Wq, L0_xattn_bq, L0_xattn_Wk, L0_xattn_bk, L0_xattn_Wv, L0_xattn_bv, L0_xattn_Wo, L0_xattn_bo, L0_ffn_gate_w, L0_ffn_W1, L0_ffn_b1, L0_ffn_W2, L0_ffn_b2, L0_ffn_sW1, L0_ffn_sb1, L0_ffn_sW2, L0_ffn_sb2):
    import jax
    import jax.numpy as jnp

    def _L0_xattn_ref(q_in, k_in, v_in, key_padding_mask, Wq, bq, Wk, bk, Wv, bv, Wo, bo):
        import jax, jax.numpy as jnp
        import numpy as np
        DIM = 256
        N_HEAD = 16
        BS, QLEN, KLEN = (4, 512, 512)
        bs, q_len, _ = q_in.shape
        k_len = k_in.shape[1]
        h = N_HEAD
        d = DIM // h
        q = (q_in @ Wq + bq).reshape(bs, q_len, h, d).transpose(0, 2, 1, 3)
        k = (k_in @ Wk + bk).reshape(bs, k_len, h, d).transpose(0, 2, 1, 3)
        v = (v_in @ Wv + bv).reshape(bs, k_len, h, d).transpose(0, 2, 1, 3)
        score = jnp.einsum('bhqd,bhkd->bhqk', q, k) / jnp.sqrt(jnp.float32(d))
        mask = key_padding_mask[:, None, None, :]
        score = jnp.where(mask, jnp.float32(-1e+30), score)
        attn = jax.nn.softmax(score, axis=-1)
        out = jnp.einsum('bhqk,bhkd->bhqd', attn, v).transpose(0, 2, 1, 3).reshape(bs, q_len, DIM)
        return out @ Wo + bo

    def _L0_ffn_ref(x, gate_w, W1, b1, W2, b2, sW1, sb1, sW2, sb2):
        import jax, jax.numpy as jnp
        import numpy as np
        TOP_K = 2
        B, S, H = x.shape
        E = gate_w.shape[0]
        x_flat = x.reshape(-1, H)
        logits = x_flat @ gate_w.T
        probs = jax.nn.softmax(logits.astype(jnp.float32), axis=-1)
        top_w, sel = jax.lax.top_k(probs, TOP_K)
        top_w = top_w / jnp.sum(top_w, axis=-1, keepdims=True)
        combine = jnp.sum(jax.nn.one_hot(sel, E, dtype=top_w.dtype) * top_w[..., None], axis=1)
        combine = combine.astype(x.dtype)
        h = jax.nn.gelu(jnp.einsum('th,ehf->tef', x_flat, W1) + b1[None], approximate=False)
        y = jnp.einsum('tef,efh->teh', h, W2) + b2[None]
        out = jnp.einsum('teh,te->th', y, combine)
        sh = jax.nn.gelu(x_flat @ sW1 + sb1, approximate=False)
        out = out + sh @ sW2 + sb2
        return out.reshape(B, S, H)
    x = x + jnp.tanh(g_xattn[0]) * _L0_xattn_ref(_layernorm(x, axis=-1), ctx_1024, ctx_1024, mask_BxS2_bf0, L0_xattn_Wq, L0_xattn_bq, L0_xattn_Wk, L0_xattn_bk, L0_xattn_Wv, L0_xattn_bv, L0_xattn_Wo, L0_xattn_bo)
    x = x + jnp.tanh(g_ffn[0]) * _L0_ffn_ref(_layernorm(x, axis=-1), L0_ffn_gate_w, L0_ffn_W1, L0_ffn_b1, L0_ffn_W2, L0_ffn_b2, L0_ffn_sW1, L0_ffn_sb1, L0_ffn_sW2, L0_ffn_sb2)
    return x

_drawn_inputs = setup_inputs


def setup_inputs(seed=0):
    import zlib

    import numpy as np

    out = dict(_drawn_inputs(seed))
    spreads = {'L0_xattn_bq': (0.0, 0.1),
     'L0_xattn_bk': (0.0, 0.1),
     'L0_xattn_bv': (0.0, 0.1),
     'L0_xattn_bo': (0.0, 0.1),
     'L0_ffn_b1': (0.0, 0.1),
     'L0_ffn_b2': (0.0, 0.1),
     'L0_ffn_sb1': (0.0, 0.1),
     'L0_ffn_sb2': (0.0, 0.1)}
    factors = {}
    for name, (base, spread) in spreads.items():
        noise = np.random.default_rng([zlib.crc32(name.encode()), seed]).standard_normal(out[name].shape)
        drawn = base * np.exp(spread * noise) if base else spread * noise
        out[name] = jnp.asarray(drawn.astype(out[name].dtype))
    for name, factor in factors.items():
        out[name] = (out[name] * factor).astype(out[name].dtype)
    return out
```

```python
from contextlib import ExitStack

import concourse.bass as bass
from concourse import mybir

F32 = mybir.dt.float32
F32R = mybir.dt.float32r
BF16 = mybir.dt.bfloat16
I32 = mybir.dt.int32
U8 = mybir.dt.uint8
ALU = mybir.AluOpType
ACT = mybir.ActivationFunctionType
AX_X = mybir.AxisListType.X

P = 128
EPS = 1e-5
MASKED = -4e30
FAR = 99.0


def each(engine, first, end, body):
    if end - first == 1:
        body(first)
    elif end > first:
        with engine.Fori(first, end) as i:
            body(i)


def gated_cross_attention_and_moe(
    nc, x, ctx, mask, g_xattn, g_ffn, Wq, bq, Wk, bk, Wv, bv, Wo, bo,
    gate_w, W1, b1, W2, b2, sW1, sb1, sW2, sb2, out,
):
    B, SQ, D = x.shape
    SK = ctx.shape[1]
    H = 16
    DH = D // H
    E, _, F = W1.shape
    NT = B * SQ // P
    TB = SQ // P
    C = D // P
    FC = F // P
    HC = H // C
    CTX = B * SK
    SCALE = float(DH) ** -0.5
    assert (P, TB, C, HC * DH) == (128, 2, 2, P) and MASKED * SCALE == -1e30

    TOP = 2
    NA = NT // 2
    NB = NT - NA
    NR = (TOP * NT * P + E * (P - 1)) // P
    TILES = NA + NR + NB
    R0, R1 = NA, NA + NR
    PH = E + 2

    rows = nc.dram_tensor("ffn_rows", (TILES * P, D), F32, kind="Internal").ap()
    routed_y = nc.dram_tensor("routed_y", (NR * P, D), F32, kind="Internal").ap()
    x_v = x.rearrange("b (j p) d -> p (b j) d", p=P)
    out_v = out.rearrange("b (j p) d -> p (b j) d", p=P)
    ctx_v = ctx.rearrange("b k d -> (b k) d")
    rows_v = rows.rearrange("(t p) d -> t p d", p=P)
    y_v = routed_y.rearrange("(t p) d -> t p d", p=P)
    chunked = lambda w: w.rearrange("(c p) n -> p c n", p=P)
    W1_v = W1.rearrange("e (c p) f -> e p c f", p=P)
    W2_v = W2.rearrange("e (c p) h -> e p c h", p=P)

    with ExitStack() as stack:
        def sb(name, shape, dt=F32, where=stack):
            return where.enter_context(nc.sbuf_tensor(name, shape, dt))

        def sem(name):
            return stack.enter_context(nc.semaphore(name))

        xres = sb("xres", [P, NT, D])
        x2all = sb("x2all", [P, NT, D])
        w1h = sb("w1h", [P, 2, C, F], F32R)
        w1l = sb("w1l", [P, 2, C, F], F32R)
        w2hl = sb("w2hl", [P, 2, FC, 2 * D], F32R)
        b1bc = sb("b1bc", [P, 2, F])
        b2bc = sb("b2bc", [P, 2, D])
        stage1 = sb("stage1", [P, C, F])
        stage2 = sb("stage2", [P, FC, D])
        ident = sb("ident", [P, P])
        ones = sb("ones", [P, P])
        before = sb("before", [P, P])
        zeros = sb("zeros", [P, D])
        ones_bf = sb("ones_bf", [1, P], BF16)
        eps = sb("eps", [P, 1])
        gates = sb("gates", [P, 2])
        tgate = sb("tgate", [P, 2])
        logits = sb("logits", [P, NT, E])
        slot_y = sb("slot_y", [P, TOP, NT], I32)
        slot_x = sb("slot_x", [P, TOP, NT], I32)
        share = sb("share", [P, TOP, NT])
        phase_of = sb("phase_of", [1, TILES], I32)
        first_tile = sb("first_tile", [1, PH], I32)
        xrow = sb("xrow", [P, D])
        xTh = sb("xTh", [P, C, P], F32R)
        xTl = sb("xTl", [P, C, P], F32R)
        hid = sb("hid", [P, 2, F // 2])
        hTh = sb("hTh", [P, FC, P], F32R)
        hTl = sb("hTl", [P, FC, P], F32R)
        yrow = sb("yrow", [P, D])
        ysum = sb("ysum", [P, D])

        attn = ExitStack()
        a = lambda name, shape, dt=F32: sb(name, shape, dt, attn)
        wq, wk, wv, wo = (a(n, [P, C, D]) for n in ("wq", "wk", "wv", "wo"))
        bqT, bkT = a("bqT", [P, C]), a("bkT", [P, C])
        bv_bc, bo_bc = a("bv_bc", [P, D]), a("bo_bc", [P, D])
        gate_r = a("gate_r", [E, D])
        gateT = a("gateT", [P, C, E])
        headmask = a("headmask", [P, HC])
        mask_u8 = a("mask_u8", [1, CTX], U8)
        mask_bf = a("mask_bf", [1, CTX], BF16)
        NCT = (CTX + P - 1) // P
        front = a("front", [P, NCT * D])
        ctx_r = front[:].rearrange("p (t d) -> p t d", d=D)
        ctxT = a("ctxT", [P, C, CTX])
        kT = a("kT", [P, C, CTX])
        kdiag = a("kdiag", [P, 2, C, HC, SK])
        vals = a("vals", [SK, B, H, DH + 1])
        stats = a("stats", [P, NT, 6])
        mv = a("mv", [P, NT, 2])
        lnv = a("lnv", [P, NT])
        rstd = a("rstd", [P, NT])
        nw = a("nw", [P, 3, NT])
        xn = a("xn", [P, D])
        xnT = a("xnT", [P, C, P])
        qT = a("qT", [P, C, P])
        smax = a("smax", [P, H])
        prob = front[:, 0:H * SK].rearrange("p (h k) -> p h k", k=SK)
        probT = a("probT", [SK, 2, HC, P])
        rsum = a("rsum", [P, H])
        o_n = a("o_n", [P, D])
        oT = a("oT", [P, C, P])
        st2 = a("st2", [P, 6])
        mv2 = a("mv2", [P, 2])
        lnv2 = a("lnv2", [P, 1])
        r2 = a("r2", [P, 1])
        nw2 = a("nw2", [P, 4])
        x2 = a("x2", [P, D])
        x2T = a("x2T", [P, C, P])
        attn.close()

        gath = sb("gath", [P, NT, TOP, D])
        TE = [P, NT, E]
        iota_i = sb("iota_i", TE, I32)
        iota_e = sb("iota_e", TE)
        tile_i = sb("tile_i", [1, TILES, PH - 1], I32)
        tile_f = sb("tile_f", [1, TILES, PH - 1])
        top = sb("top", [P, TOP, NT])
        pick = sb("pick", [P, TOP, NT])
        hot = sb("hot", [P, TOP, NT, E])
        rt = sb("rt", TE)
        lg2 = sb("lg2", TE)
        chosen = sb("chosen", TE)
        cum = sb("cum", [P, 2, NT, E])
        place = sb("place", TE)
        cnt_i = sb("cnt_i", [P, E], I32)
        etiles = sb("etiles", [P, 3, E])
        starts = sb("starts", [1, PH])
        started = sb("started", [1, TILES, PH - 1])
        phase_f = sb("phase_f", [1, TILES])
        posf = sb("posf", [P, TOP, NT])
        wexp = sb("wexp", [P, 4, NT])

        ps = stack.enter_context(nc.psum_tensor("ps", [P, 8, 512], F32))
        HG = (6, 6, 4)
        p_s12 = ps[:, 0:2, 0:HG[0] * SK].rearrange("p n (h k) -> p n h k", k=SK)
        p_s3 = ps[:, 2, 0:HG[2] * SK].rearrange("p (h k) -> p h k", k=SK)
        H12 = HG[0] + HG[1]
        score_parts = ((0, 0, 6, 0, 0), (0, 6, 8, 1, 0), (1, 0, 4, 1, 2 * SK), (1, 4, 8, 2, 0))
        p_t = ps[0:SK, 3:5, :].rearrange("p n (h q) -> p (n h) q", q=P)
        p_in = ps[:, 5, 0:D]
        p_l = ps[:, 5, 0:E]
        p_wo = ps[:, 6, 0:D]
        p_o = ps[:, 7, 0:H * (DH + 1)].rearrange("p (h d) -> p h d", d=DH + 1)
        k_banks, v_banks = (0, 1, 2, 5), (3, 4, 6, 7)
        p_h = ps[:, 0:2, :]
        p_hT = ps[:, 2:4, :].rearrange("p n (c q) -> p n c q", q=P)
        p_y = ps[:, 4, :]
        p_x = ps[:, 5, 0:D].rearrange("p (c q) -> p c q", q=P)
        p_rank = ps[:, 7, 0:NT * E]
        p_tot = ps[:, 7, NT * E:2 * NT * E]

        names = """consts x_in0 x_in1 ctx_in w_in small_in zero_set rows_zeroed gate_tanh
            ctxT_ps ctxT_sb kT_ps kT_sb v_ps v_sb mask_set gT_ps gT_sb
            ln_stats ln_mv ln_log ln_rstd ln_newton
            kd_ready xn_ready xnT_ps xnT_sb q_ps q_sb s_ps s_max p_sub p_exp pt_ps pt_sb pv_half
            o_sum o_norm oT_ps oT_sb wo_ps x1_mid x1_done st2_done mv2_done ln2_log r2_done
            nw_a nw_b nw_c nw_d x2_ready x2_out x2T_ps x2T_sb l_ps l_sb
            route chosen_set rank_ps share_in share_exp tables_set slots_set scattered
            stage1_in stage2_in bias_in split_hi split_w1 split_w2 w_ready
            xrow_in xT_ps xT_hi xT_lo h_ps h_add h_act hT_ps hT_hi hT_lo y_ps y_mid y_sum y_done y_stored
            g_mid out_ready out_stored""".split()
        S = {n: sem(n) for n in names}
        g_in = [sem(f"g_in{j}") for j in range(NB)]
        block = stack.enter_context(nc.Block())

        def met(engine):
            engine.wait_ge(S["zero_set"], 1)

        @block.sync
        def _(sp):
            sp.dma_start(ctx_r[:, 0:NCT - 1, :],
                         ctx_v[0:(NCT - 1) * P, :].rearrange("(t p) d -> p t d", p=P)).then_inc(S["ctx_in"], 16)
            sp.dma_start(ctx_r[0:CTX - (NCT - 1) * P, NCT - 1, :],
                         ctx_v[(NCT - 1) * P:CTX, :]).then_inc(S["ctx_in"], 16)
            for dst, src in ((wk, Wk), (wv, Wv), (wq, Wq), (wo, Wo)):
                sp.dma_start(dst[:], chunked(src)).then_inc(S["w_in"], 16)
            sp.dma_start(xres[:, 0:4, :], x_v[:, 0:4, :]).then_inc(S["x_in0"], 16)
            sp.dma_start(xres[:, 4:NT, :], x_v[:, 4:NT, :]).then_inc(S["x_in1"], 16)
            sp.wait_ge(S["zero_set"], 1)
            sp.dma_start(rows_v[R0:R1].rearrange("t p d -> p t d"),
                         zeros[:].unsqueeze(1).to_broadcast([P, NR, D])).then_inc(S["rows_zeroed"], 16)

            def keep_x2(t, row):
                sp.wait_ge(S["x2_ready"], t + 1)
                sp.dma_start(rows_v[bass.ds(row, 1)].rearrange("o p d -> (o p) d"), x2[:]).then_inc(S["x2_out"], 16)
                sp.dma_start(x2all[:, bass.ds(t, 1), :].rearrange("p o d -> p (o d)"), x2[:]).then_inc(S["x2_out"], 16)

            each(sp, 0, NA, lambda t: keep_x2(t, t))
            each(sp, NA, NT, lambda t: keep_x2(t, t + NR))
            sp.wait_ge(S["x2_out"], 32 * NT)

            def load_rows(i):
                if not isinstance(i, int) or i:
                    sp.wait_ge(S["xT_ps"], i)
                sp.dma_start(xrow[:], rows_v[bass.ds(i, 1)].rearrange("o p d -> (o p) d")).then_inc(S["xrow_in"], 16)

            load_rows(0)
            each(sp, 1, R0, load_rows)
            sp.wait_ge(S["scattered"], 16 * TOP * NT)
            each(sp, R0, TILES, load_rows)

            def store_out(j):
                sp.wait_ge(S["out_ready"], TOP * j + TOP)
                sp.dma_start(out_v[:, bass.ds(2 * j, 2), :], xres[:, bass.ds(2 * j, 2), :]).then_inc(S["out_stored"], 16)

            each(sp, 0, NB - 1, store_out)
            sp.wait_ge(S["y_done"], NT)
            store_out(NB - 1)
            sp.wait_ge(S["out_stored"], 16 * NB)
            sp.wait_ge(S["rows_zeroed"], 16)

        @block.gpsimd
        def _(pool):
            def load_w1(p, src):
                pool.dma_start(stage1[:], src).then_inc(S["stage1_in"], 16)

            def load_w2(p, src):
                pool.dma_start(stage2[:], src).then_inc(S["stage2_in"], 16)

            sW1_v, sW2_v = chunked(sW1), chunked(sW2)
            pool.memset(ident[:], 0.0).then_inc(S["consts"], 1)
            pool.memset(ones[:], 1.0).then_inc(S["consts"], 1)
            pool.memset(before[:], 1.0).then_inc(S["consts"], 1)
            pool.memset(headmask[:], 1.0).then_inc(S["consts"], 1)
            pool.wait_ge(S["consts"], 4)
            pool.affine_select(out=ident[:], in_=ident[:], compare_op=ALU.not_equal, fill=1.0, base=0,
                               pattern=[[-1, P]], channel_multiplier=1).then_inc(S["consts"], 1)
            pool.affine_select(out=before[:], in_=before[:], compare_op=ALU.is_gt, fill=0.0, base=0,
                               pattern=[[1, P]], channel_multiplier=-1).then_inc(S["consts"], 1)
            pool.affine_select(out=headmask[:], in_=headmask[:], compare_op=ALU.is_ge, fill=0.0, base=0,
                               pattern=[[-DH, HC]], channel_multiplier=1).then_inc(S["consts"], 1)
            pool.wait_ge(S["consts"], 7)
            pool.affine_select(out=headmask[:], in_=headmask[:], compare_op=ALU.is_ge, fill=0.0, base=DH - 1,
                               pattern=[[DH, HC]], channel_multiplier=-1).then_inc(S["consts"], 1)
            load_w1(0, sW1_v)
            load_w2(0, sW2_v)
            pool.wait_ge(S["consts"], 8)
            pool.wait_ge(S["kT_sb"], 2 * C)

            def key_diag(b):
                if b >= 2:
                    pool.wait_ge(S["s_ps"], TB * (b - 1))
                for c in range(C):
                    pool.tensor_tensor(
                        kdiag[:, b % 2, c, :, :],
                        kT[:, c, b * SK:(b + 1) * SK].unsqueeze(1).to_broadcast([P, HC, SK]),
                        headmask[:].unsqueeze(2).to_broadcast([P, HC, SK]), ALU.mult).then_inc(S["kd_ready"], 1)

            def split_w1(p, s):
                pool.wait_ge(S["stage1_in"], 16 * p + 16)
                hi = w1h[:, bass.ds(s, 1), :, :].rearrange("p o c f -> p (o c) f")
                lo = w1l[:, bass.ds(s, 1), :, :].rearrange("p o c f -> p (o c) f")
                pool.tensor_tensor(hi, stage1[:], zeros[:, 0:1].unsqueeze(2).to_broadcast([P, C, F]),
                                   ALU.add).then_inc(S["split_hi"], 1)
                pool.wait_ge(S["split_hi"], 2 * p + 1)
                pool.tensor_tensor(lo, stage1[:], hi.bitcast(F32), ALU.subtract).then_inc(S["split_w1"], 1)
                met(pool)
                pool.wait_ge(S["split_w1"], p + 1)

            def split_w2(p, s):
                pool.wait_ge(S["stage2_in"], 16 * p + 16)
                both = w2hl[:, bass.ds(s, 1), :, :].rearrange("p o c f -> p (o c) f")
                pool.tensor_tensor(both[:, :, 0:D], stage2[:], zeros[:, 0:1].unsqueeze(2).to_broadcast([P, FC, D]),
                                   ALU.add).then_inc(S["split_hi"], 1)
                pool.wait_ge(S["split_hi"], 2 * p + 2)
                pool.tensor_tensor(both[:, :, D:2 * D], stage2[:], both[:, :, 0:D].bitcast(F32),
                                   ALU.subtract).then_inc(S["split_w2"], 1)
                met(pool)
                pool.wait_ge(S["split_w2"], p + 1)

            def biases(s, first, second):
                pool.dma_start(b1bc[:, bass.ds(s, 1), :].rearrange("p o f -> p (o f)"), first).then_inc(S["bias_in"], 16)
                pool.dma_start(b2bc[:, bass.ds(s, 1), :].rearrange("p o f -> p (o f)"), second).then_inc(S["bias_in"], 16)

            def phase_ready(p):
                pool.wait_ge(S["bias_in"], 32 * p + 32)
                pool.sem_inc(S["w_ready"], 1)

            shared_b = (sb1.partition_broadcast(P), sb2.partition_broadcast(P))
            expert_b = lambda e: (b1[bass.ds(e, 1), :].rearrange("o f -> (o f)").partition_broadcast(P),
                                  b2[bass.ds(e, 1), :].rearrange("o f -> (o f)").partition_broadcast(P))
            expert_w1 = lambda e: W1_v[bass.ds(e, 1)].rearrange("o p c f -> p (o c) f")
            expert_w2 = lambda e: W2_v[bass.ds(e, 1)].rearrange("o p c f -> p (o c) f")

            pool.wait_ge(S["zero_set"], 1)
            key_diag(0)
            key_diag(1)
            biases(0, *shared_b)
            split_w1(0, 0)
            load_w1(1, expert_w1(0))
            key_diag(2)
            split_w2(0, 0)
            load_w2(1, expert_w2(0))
            phase_ready(0)
            key_diag(3)
            biases(1, *expert_b(0))
            split_w1(1, 1)
            load_w1(2, expert_w1(1))
            key_diag(4)
            split_w2(1, 1)
            load_w2(2, expert_w2(1))
            phase_ready(1)
            for b in range(5, B):
                key_diag(b)
            pool.wait_ge(S["l_sb"], NT)
            pool.iota(iota_i[:], pattern=[[0, NT], [1, E]], base=0, channel_multiplier=0).then_inc(S["route"], 1)
            pool.iota(tile_i[:], pattern=[[1, TILES], [0, PH - 1]], base=0, channel_multiplier=0).then_inc(S["route"], 1)

            pool.wait_ge(S["slots_set"], 1)
            pool.wait_ge(S["rows_zeroed"], 16)
            pool.wait_ge(S["x2_out"], 32 * NT)
            for t in range(NT):
                for k in range(TOP):
                    pool.indirect_dma_start(
                        out=rows, out_offset=bass.IndirectOffsetOnAxis(ap=slot_x[:, k, t:t + 1], axis=0),
                        in_=x2all[:, t, :], in_offset=None).then_inc(S["scattered"], 16)

            def phase(p, s, bias, ahead):
                first = pool.value_load(first_tile[0:1, bass.ds(p - 1, 1)], min_val=R0, max_val=R1)
                met(pool)
                pool.wait_ge(S["y_sum"], first)
                biases(s, *bias)
                split_w1(p, s)
                if ahead:
                    load_w1(p + 1, ahead[0])
                split_w2(p, s)
                if ahead:
                    load_w2(p + 1, ahead[1])
                phase_ready(p)

            pool.wait_ge(S["tables_set"], 1)
            with pool.Fori(2, E) as p:
                phase(p, p % 2, expert_b(p - 1), (expert_w1(p), expert_w2(p)))
            phase(E, E % 2, expert_b(E - 1), (sW1_v, sW2_v))
            phase(E + 1, (E + 1) % 2, shared_b, None)

            pool.wait_ge(S["y_stored"], 16 * NR)
            for t in range(NT):
                for k in range(TOP):
                    pool.indirect_dma_start(
                        out=gath[:, t, k, :], out_offset=None, in_=routed_y,
                        in_offset=bass.IndirectOffsetOnAxis(ap=slot_y[:, k, t:t + 1], axis=0)
                    ).then_inc(g_in[t // 2], 16)

        @block.tensor
        def _(pe):
            mm = nc.tensor.matmul
            pe.wait_ge(S["consts"], 5)
            pe.wait_ge(S["ctx_in"], 32)
            for k in range(NCT):
                n = min(P, CTX - k * P)
                dst = ps[:, k, :]
                for c in range(C):
                    last = nc.tensor.transpose(dst[:, c * P:c * P + n], ctx_r[0:n, k, c * P:(c + 1) * P],
                                               ident[0:n, 0:n])
                last.then_inc(S["ctxT_ps"], 1)
            pe.wait_ge(S["w_in"], 64)
            pe.wait_ge(S["ctxT_sb"], NCT)
            HALF = CTX // 2
            for co in range(C):
                for n in range(2):
                    for ci in range(C):
                        last = mm(ps[:, k_banks[2 * co + n], 0:HALF], wk[:, ci, co * P:(co + 1) * P],
                                  ctxT[:, ci, n * HALF:(n + 1) * HALF], start=ci == 0, stop=ci == C - 1)
                    last.then_inc(S["kT_ps"], 1)
            for b in range(B):
                dst = ps[0:SK, v_banks[b // 2], :]
                for ci in range(C):
                    last = mm(dst[:, (b % 2) * D:(b % 2 + 1) * D], ctxT[:, ci, b * SK:(b + 1) * SK], wv[:, ci, :],
                              start=ci == 0, stop=ci == C - 1)
                if b % 2:
                    last.then_inc(S["v_ps"], 1)
            pe.wait_ge(S["small_in"], 16 * 8)
            pe.wait_ge(S["v_sb"], B // 2)
            for c in range(C):
                last = nc.tensor.transpose(ps[:, 7, c * E:(c + 1) * E], gate_r[:, c * P:(c + 1) * P],
                                           ident[0:E, 0:E])
            last.then_inc(S["gT_ps"], 1)
            pe.wait_ge(S["gT_sb"], 1)

            def norm_in(t):
                pe.wait_ge(S["xn_ready"], t + 1)
                for c in range(C):
                    last = nc.tensor.transpose(p_in[:, c * P:(c + 1) * P], xn[:, c * P:(c + 1) * P], ident[:])
                last.then_inc(S["xnT_ps"], 1)

            def queries(t):
                pe.wait_ge(S["xnT_sb"], t + 1)
                for co in range(C):
                    for ci in range(C):
                        last = mm(p_in[:, co * P:(co + 1) * P], wq[:, ci, co * P:(co + 1) * P], xnT[:, ci, :],
                                  start=ci == 0, stop=ci == C - 1)
                last.then_inc(S["q_ps"], 1)

            def scores(t):
                if not isinstance(t, int) or t >= 1:
                    pe.wait_ge(S["p_sub"], t)
                pe.wait_ge(S["q_sb"], t + 1)
                b = t // TB
                pe.wait_ge(S["kd_ready"], C * (b + 1))
                for c, h0, h1, n, col in score_parts:
                    dst = ps[:, n, col:col + (h1 - h0) * SK]
                    keys = kdiag[:, bass.ds(b % 2, 1), c, h0:h1, :]
                    mm(dst, qT[:, c, :], keys.rearrange("p o h k -> p (o h k)"), start=True, stop=False)
                    masked = mask_bf[0:1, bass.ds(b * SK, SK)].unsqueeze(1).to_broadcast([1, h1 - h0, SK])
                    last = mm(dst, ones_bf[0:1, :], masked, start=False, stop=True)
                last.then_inc(S["s_ps"], 1)

            def turn_probs(t, c):
                if c == 0:
                    pe.wait_ge(S["p_exp"], t + 1)
                    if not isinstance(t, int) or t >= 1:
                        pe.wait_ge(S["pt_sb"], 2 * t)
                else:
                    pe.wait_ge(S["pt_sb"], 2 * t + 1)
                for h in range(HC):
                    last = nc.tensor.transpose(p_t[:, h, :], prob[:, c * HC + h, :], ident[:])
                last.then_inc(S["pt_ps"], 1)

            def attend(t, c):
                pe.wait_ge(S["pt_sb"], 2 * t + c + 1)
                if c == 0 and (not isinstance(t, int) or t >= 1):
                    pe.wait_ge(S["o_norm"], t)
                for h in range(HC):
                    last = mm(p_o[:, c * HC + h, :], probT[:, c, h, :],
                              vals[:, bass.ds(t // TB, 1), c * HC + h, :].rearrange("k o d -> k (o d)"),
                              start=True, stop=True)
                last.then_inc(S["pv_half"], 1)

            def turn_heads(t):
                pe.wait_ge(S["o_norm"], t + 1)
                if not isinstance(t, int) or t >= 1:
                    pe.wait_ge(S["x1_mid"], t)
                for c in range(C):
                    last = nc.tensor.transpose(p_wo[:, c * P:(c + 1) * P], o_n[:, c * P:(c + 1) * P], ident[:])
                last.then_inc(S["oT_ps"], 1)

            def project(t):
                pe.wait_ge(S["oT_sb"], t + 1)
                for c in range(C):
                    last = mm(p_wo, oT[:, c, :], wo[:, c, :], start=c == 0, stop=c == C - 1)
                last.then_inc(S["wo_ps"], 1)

            def turn_x2(t):
                pe.wait_ge(S["x2_ready"], t + 1)
                for c in range(C):
                    last = nc.tensor.transpose(p_in[:, c * P:(c + 1) * P], x2[:, c * P:(c + 1) * P], ident[:])
                last.then_inc(S["x2T_ps"], 1)

            def route_logits(t):
                pe.wait_ge(S["x2T_sb"], t + 1)
                for c in range(C):
                    last = mm(p_l, x2T[:, c, :], gateT[:, c, :], start=c == 0, stop=c == C - 1)
                last.then_inc(S["l_ps"], 1)

            def step(t):
                known = isinstance(t, int)
                ok = lambda u: not known or 0 <= u < NT
                if ok(t - 3):
                    pe.wait_ge(S["q_sb"], t + 2 if ok(t + 1) else NT)
                    route_logits(t - 3)
                if ok(t + 1):
                    scores(t + 1)
                if ok(t - 2):
                    if ok(t - 3):
                        pe.wait_ge(S["l_sb"], t - 2)
                    turn_x2(t - 2)
                if ok(t):
                    turn_probs(t, 0)
                if ok(t - 1):
                    turn_heads(t - 1)
                if ok(t):
                    attend(t, 0)
                if ok(t + 2):
                    if ok(t - 2):
                        pe.wait_ge(S["x2T_sb"], t - 1)
                    norm_in(t + 2)
                if ok(t):
                    turn_probs(t, 1)
                if ok(t - 1):
                    project(t - 1)
                if ok(t + 2):
                    queries(t + 2)
                if ok(t):
                    attend(t, 1)

            pe.wait_ge(S["kT_sb"], 2 * C)
            norm_in(0)
            queries(0)
            pe.wait_ge(S["q_sb"], 1)
            norm_in(1)
            pe.wait_ge(S["mask_set"], 2)
            scores(0)
            queries(1)
            step(0)
            step(1)
            step(2)
            each(pe, 3, NT - 2, step)
            for t in range(NT - 2, NT + 3):
                step(t)

            def ranks():
                pe.wait_ge(S["chosen_set"], 1)
                moving = chosen[:].rearrange("p t e -> p (t e)")
                mm(p_rank, before[:], moving, start=True, stop=True)
                mm(p_tot, ones[:], moving, start=True, stop=True).then_inc(S["rank_ps"], 1)

            def turn_rows(i):
                pe.wait_ge(S["xrow_in"], 16 * i + 16)
                for c in range(C):
                    last = nc.tensor.transpose(p_x[:, c, :], xrow[:, c * P:(c + 1) * P], ident[:])
                last.then_inc(S["xT_ps"], 1)

            def turn_hidden(i):
                for n in range(2):
                    pe.wait_ge(S["h_act"], 2 * i + n + 1)
                    for c in range(FC // 2):
                        last = nc.tensor.transpose(p_hT[:, n, c, :], hid[:, n, c * P:(c + 1) * P], ident[:])
                    last.then_inc(S["hT_ps"], 1)

            def up(i, p, s):
                pe.wait_ge(S["w_ready"], p + 1)
                pe.wait_ge(S["xT_lo"], i + 1)
                for n in range(2):
                    if not isinstance(i, int) or i >= 1:
                        pe.wait_ge(S["h_add"], 2 * i - 1 + n)
                    part = lambda w, c: w[:, bass.ds(s, 1), c, n * (F // 2):(n + 1) * (F // 2)].rearrange(
                        "p o f -> p (o f)")
                    for c in range(C):
                        mm(p_h[:, n, :], xTh[:, c, :], part(w1l, c), start=c == 0, stop=False)
                        mm(p_h[:, n, :], xTh[:, c, :], part(w1h, c), start=False, stop=False)
                        last = mm(p_h[:, n, :], xTl[:, c, :], part(w1h, c), start=False, stop=c == C - 1)
                    last.then_inc(S["h_ps"], 1)

            def down(i, s):
                pe.wait_ge(S["hT_lo"], 2 * i + 2)
                if not isinstance(i, int) or i >= 1:
                    pe.wait_ge(S["y_sum"], i)
                for c in range(FC):
                    part = lambda n: w2hl[:, bass.ds(s, 1), c, 0:n].rearrange("p o f -> p (o f)")
                    mm(p_y, hTh[:, c, :], part(2 * D), start=c == 0, stop=False)
                    last = mm(p_y[:, 0:D], hTl[:, c, :], part(D), start=False, stop=c == FC - 1)
                last.then_inc(S["y_ps"], 1)

            def phase_at(i):
                if isinstance(i, int) and i < R0:
                    return 0, 0
                if isinstance(i, int) and i >= R1:
                    return PH - 1, (PH - 1) % 2
                p = pe.value_load(phase_of[0:1, bass.ds(i, 1)], min_val=0, max_val=PH - 1)
                return p, p % 2

            def tile(i, now=None, last=None):
                known = isinstance(i, int)
                if not known or i >= 1:
                    turn_hidden(i - 1)
                if not known or i < TILES:
                    up(i, *(now or phase_at(i)))
                if not known or i < TILES - 1:
                    turn_rows(i + 1)
                if not known or i >= 1:
                    down(i - 1, (last or phase_at(i - 1))[1])

            pe.wait_ge(S["l_sb"], NT)
            turn_rows(0)
            tile(0)
            ranks()
            each(pe, 1, R0, lambda i: tile(i, (0, 0), (0, 0)))
            pe.wait_ge(S["tables_set"], 2)
            tile(R0)
            each(pe, R0 + 1, TILES - 1, tile)
            tile(TILES - 1)
            tile(TILES)

        @block.scalar
        def _(act):
            for dst, src in ((bqT, bq), (bkT, bk)):
                act.dma_start(dst[:], src.rearrange("(c p) -> p c", p=P), allow_slow_non_contiguous=True
                              ).then_inc(S["small_in"], 16)
            act.dma_start(bv_bc[:], bv.partition_broadcast(P)).then_inc(S["small_in"], 16)
            act.dma_start(bo_bc[:], bo.partition_broadcast(P)).then_inc(S["small_in"], 16)
            act.dma_start(gate_r[:], gate_w).then_inc(S["small_in"], 16)
            act.dma_start(mask_u8[:], mask.rearrange("b k -> (b k)").unsqueeze(0)).then_inc(S["small_in"], 16)
            act.dma_start(gates[:, 0:1], g_xattn.partition_broadcast(P)).then_inc(S["small_in"], 16)
            act.dma_start(gates[:, 1:2], g_ffn.partition_broadcast(P)).then_inc(S["small_in"], 16)
            act.wait_ge(S["small_in"], 16 * 8)
            act.activation(tgate[:], gates[:], ACT.Tanh).then_inc(S["gate_tanh"], 1)
            act.preload_act_table_set("natural_log_exp_and_others")
            for k in range(NCT):
                n = min(P, CTX - k * P)
                src = ps[:, k, :]
                act.wait_ge(S["ctxT_ps"], k + 1)
                act.activation(ctxT[:, :, k * P:k * P + n],
                               src[:, 0:C * P].rearrange("p (c q) -> p c q", q=P)[:, :, 0:n],
                               ACT.Copy).then_inc(S["ctxT_sb"], 1)
            for co in range(C):
                for n in range(2):
                    act.wait_ge(S["kT_ps"], 2 * co + n + 1)
                    act.activation(kT[:, co, n * CTX // 2:(n + 1) * CTX // 2], ps[:, k_banks[2 * co + n], 0:CTX // 2],
                                   ACT.Identity, bias=bkT[:, co:co + 1]).then_inc(S["kT_sb"], 1)
            act.wait_ge(S["ln_mv"], NT)
            act.activation(lnv[:], mv[:, :, 1], ACT.Ln, bias=eps[:, 0:1]).then_inc(S["ln_log"], 1)
            act.wait_ge(S["ln_log"], 1)
            act.activation(rstd[:], lnv[:], ACT.Exp, scale=-0.5).then_inc(S["ln_rstd"], 1)

            def norm_in(t):
                act.wait_ge(S["xnT_ps"], t + 1)
                act.activation(xnT[:].rearrange("p c q -> p (c q)"), p_in, ACT.Copy).then_inc(S["xnT_sb"], 1)

            def queries(t):
                act.wait_ge(S["q_ps"], t + 1)
                if not isinstance(t, int) or t >= 1:
                    act.wait_ge(S["s_ps"], t)
                for c in range(C):
                    last = act.activation(qT[:, c, :], p_in[:, c * P:(c + 1) * P], ACT.Identity, bias=bqT[:, c:c + 1])
                last.then_inc(S["q_sb"], 1)

            def exponent(t):
                act.wait_ge(S["p_sub"], t + 1)
                act.activation(front[:, 0:H * SK], front[:, 0:H * SK], ACT.Exp, scale=SCALE).then_inc(S["p_exp"], 1)

            def turned_probs(t, c):
                act.wait_ge(S["pt_ps"], 2 * t + c + 1)
                if not isinstance(t, int) or t >= 1:
                    act.wait_ge(S["pv_half"], 2 * t + c - 1)
                act.activation(probT[:, c, :, :], p_t, ACT.Copy).then_inc(S["pt_sb"], 1)

            def turned_heads(t):
                act.wait_ge(S["oT_ps"], t + 1)
                act.activation(oT[:].rearrange("p c q -> p (c q)"), p_wo, ACT.Copy).then_inc(S["oT_sb"], 1)

            def deviation(t):
                act.wait_ge(S["mv2_done"], t + 1)
                act.activation(lnv2[:], mv2[:, 1:2], ACT.Ln, bias=eps[:, 0:1]).then_inc(S["ln2_log"], 1)
                act.wait_ge(S["ln2_log"], t + 1)
                act.activation(r2[:], lnv2[:], ACT.Exp, scale=-0.5).then_inc(S["r2_done"], 1)

            def step(t):
                ok = lambda u: not isinstance(t, int) or 0 <= u < NT
                if ok(t):
                    exponent(t)
                    turned_probs(t, 0)
                if ok(t - 1):
                    turned_heads(t - 1)
                if ok(t + 2):
                    norm_in(t + 2)
                if ok(t):
                    turned_probs(t, 1)
                if ok(t + 2):
                    queries(t + 2)
                if ok(t - 1):
                    deviation(t - 1)

            norm_in(0)
            queries(0)
            norm_in(1)
            queries(1)
            step(0)
            step(1)
            each(act, 2, NT - 2, step)
            for t in range(NT - 2, NT + 1):
                step(t)

            def rows_hi(i):
                act.wait_ge(S["xT_ps"], i + 1)
                act.activation(xTh[:], p_x, ACT.Copy).then_inc(S["xT_hi"], 1)

            def hidden_hi(i):
                for n in range(2):
                    act.wait_ge(S["hT_ps"], 2 * i + n + 1)
                    act.activation(hTh[:, n * (FC // 2):(n + 1) * (FC // 2), :], p_hT[:, n, :, :],
                                   ACT.Copy).then_inc(S["hT_hi"], 1)

            def gelu(i):
                for n in range(2):
                    act.wait_ge(S["h_add"], 2 * i + n + 1)
                    act.activation(hid[:, n, :], hid[:, n, :], ACT.Gelu).then_inc(S["h_act"], 1)

            def store_y(i):
                act.wait_ge(S["y_sum"], i + 1)
                act.dma_start(y_v[bass.ds(i - R0, 1)].rearrange("o p d -> (o p) d"), yrow[:]).then_inc(S["y_stored"], 16)

            def tile(i, store=False):
                known = isinstance(i, int)
                if not known or i >= 1:
                    hidden_hi(i - 1)
                if store:
                    store_y(i - 2)
                if not known or i < TILES:
                    gelu(i)
                if not known or i < TILES - 1:
                    rows_hi(i + 1)

            rows_hi(0)
            act.wait_ge(S["share_in"], 1)
            act.activation(wexp[:, 1, :], wexp[:, 0, :], ACT.Exp).then_inc(S["share_exp"], 1)
            tile(0)
            each(act, 1, R0 + 2, tile)
            each(act, R0 + 2, R1 + 2, lambda i: tile(i, True))
            each(act, R1 + 2, TILES - 1, tile)
            tile(TILES - 1)
            tile(TILES)

        @block.vector
        def _(dve):
            tt, ts, stt = dve.tensor_tensor, dve.tensor_scalar, dve.scalar_tensor_tensor
            dve.memset(zeros[:], 0.0).then_inc(S["zero_set"], 1)
            dve.memset(eps[:], EPS)
            dve.memset(vals[:], 1.0).then_inc(S["mask_set"], 1)
            dve.memset(ones_bf[:], 1.0)
            dve.wait_ge(S["small_in"], 16 * 8)
            ts(mask_bf[:], mask_u8[:], MASKED, None, ALU.mult).then_inc(S["mask_set"], 1)
            for t in range(NT):
                if t == 0:
                    dve.wait_ge(S["x_in0"], 16)
                if t == 4:
                    dve.wait_ge(S["x_in1"], 16)
                dve.bn_stats(stats[:, t, :], xres[:, t, :]).then_inc(S["ln_stats"], 1)
            for t in range(NT):
                dve.wait_ge(S["ln_stats"], t + 1)
                dve.bn_aggr(mv[:, t, :], stats[:, t, :]).then_inc(S["ln_mv"], 1)
            dve.wait_ge(S["mask_set"], 1)
            for n in range(B // 2):
                src = ps[0:SK, v_banks[n], :]
                dve.wait_ge(S["v_ps"], n + 1)
                tt(vals[:, 2 * n:2 * n + 2, :, 0:DH],
                   src.rearrange("k (b h d) -> k b h d", b=2, d=DH),
                   bv_bc[0:SK, :].rearrange("k (h d) -> k h d", d=DH).unsqueeze(1).to_broadcast([SK, 2, H, DH]),
                   ALU.add).then_inc(S["v_sb"], 1)
            dve.wait_ge(S["gT_ps"], 1)
            dve.tensor_copy(gateT[:], ps[:, 7, 0:C * E].rearrange("p (c e) -> p c e", e=E)).then_inc(S["gT_sb"], 1)

            dve.wait_ge(S["ln_rstd"], 1)
            tt(nw[:, 0, :], rstd[:], rstd[:], ALU.mult).then_inc(S["ln_newton"], 1)
            dve.wait_ge(S["ln_newton"], 1)
            stt(nw[:, 1, :], mv[:, :, 1], EPS, nw[:, 0, :], ALU.add, ALU.mult).then_inc(S["ln_newton"], 1)
            dve.wait_ge(S["ln_newton"], 2)
            ts(nw[:, 2, :], nw[:, 1, :], -0.5, 1.5, ALU.mult, ALU.add).then_inc(S["ln_newton"], 1)
            dve.wait_ge(S["ln_newton"], 3)
            tt(rstd[:], rstd[:], nw[:, 2, :], ALU.mult).then_inc(S["ln_newton"], 1)
            dve.wait_ge(S["ln_newton"], 4)
            dve.wait_ge(S["gate_tanh"], 1)

            def col(ap, t):
                return ap[:, bass.ds(t, 1)]

            def row(ap, t):
                return ap[:, bass.ds(t, 1), :].rearrange("p o d -> p (o d)")

            def norm_in(t):
                if not isinstance(t, int) or t >= 1:
                    dve.wait_ge(S["xnT_ps"], t)
                ts(xn[:], row(xres, t), row(mv, t)[:, 0:1], col(rstd, t), ALU.subtract, ALU.mult
                   ).then_inc(S["xn_ready"], 1)

            def score_max(t):
                dve.wait_ge(S["s_ps"], t + 1)
                dve.tensor_reduce(smax[:, 0:H12].rearrange("p (n h) -> p n h", n=2), p_s12, AX_X, ALU.max)
                dve.tensor_reduce(smax[:, H12:H], p_s3, AX_X, ALU.max).then_inc(S["s_max"], 1)

            def score_sub(t):
                if not isinstance(t, int) or t >= 1:
                    dve.wait_ge(S["pt_ps"], 2 * t)
                dve.wait_ge(S["s_max"], t + 1)
                tt(prob[:, 0:H12, :].rearrange("p (n h) k -> p n h k", n=2), p_s12,
                   smax[:, 0:H12].rearrange("p (n h) -> p n h", n=2).unsqueeze(3).to_broadcast([P, 2, HG[0], SK]),
                   ALU.subtract)
                tt(prob[:, H12:H, :], p_s3, smax[:, H12:H].unsqueeze(2).to_broadcast([P, HG[2], SK]),
                   ALU.subtract).then_inc(S["p_sub"], 1)

            def normalise(t):
                dve.wait_ge(S["pv_half"], 2 * t + 2)
                dve.reciprocal(rsum[:], p_o[:, :, DH]).then_inc(S["o_sum"], 1)
                if not isinstance(t, int) or t >= 1:
                    dve.wait_ge(S["oT_ps"], t)
                dve.wait_ge(S["o_sum"], t + 1)
                tt(o_n[:].rearrange("p (h d) -> p h d", d=DH), p_o[:, :, 0:DH],
                   rsum[:].unsqueeze(2).to_broadcast([P, H, DH]), ALU.mult).then_inc(S["o_norm"], 1)

            def residual(t):
                dve.wait_ge(S["wo_ps"], t + 1)
                stt(row(xres, t), p_wo, tgate[:, 0:1], row(xres, t), ALU.mult, ALU.add).then_inc(S["x1_mid"], 1)
                dve.wait_ge(S["x1_mid"], t + 1)
                stt(row(xres, t), bo_bc[:], tgate[:, 0:1], row(xres, t), ALU.mult, ALU.add).then_inc(S["x1_done"], 1)
                met(dve)
                dve.wait_ge(S["x1_done"], t + 1)
                dve.bn_stats(st2[:], row(xres, t)).then_inc(S["st2_done"], 1)
                met(dve)
                dve.wait_ge(S["st2_done"], t + 1)
                dve.bn_aggr(mv2[:], st2[:]).then_inc(S["mv2_done"], 1)

            def norm_two(t):
                dve.wait_ge(S["r2_done"], t + 1)
                tt(nw2[:, 0:1], r2[:], r2[:], ALU.mult).then_inc(S["nw_a"], 1)
                dve.wait_ge(S["nw_a"], t + 1)
                stt(nw2[:, 1:2], mv2[:, 1:2], EPS, nw2[:, 0:1], ALU.add, ALU.mult).then_inc(S["nw_b"], 1)
                dve.wait_ge(S["nw_b"], t + 1)
                ts(nw2[:, 2:3], nw2[:, 1:2], -0.5, 1.5, ALU.mult, ALU.add).then_inc(S["nw_c"], 1)
                dve.wait_ge(S["nw_c"], t + 1)
                tt(nw2[:, 3:4], r2[:], nw2[:, 2:3], ALU.mult).then_inc(S["nw_d"], 1)
                dve.wait_ge(S["nw_d"], t + 1)
                if not isinstance(t, int) or t >= 1:
                    dve.wait_ge(S["x2_out"], 32 * t)
                    dve.wait_ge(S["x2T_ps"], t)
                ts(x2[:], row(xres, t), mv2[:, 0:1], nw2[:, 3:4], ALU.subtract, ALU.mult).then_inc(S["x2_ready"], 1)

            def turned_x2(t):
                dve.wait_ge(S["x2T_ps"], t + 1)
                if not isinstance(t, int) or t >= 1:
                    dve.wait_ge(S["l_ps"], t)
                dve.tensor_copy(x2T[:].rearrange("p c q -> p (c q)"), p_in).then_inc(S["x2T_sb"], 1)

            def keep_logits(t):
                dve.wait_ge(S["l_ps"], t + 1)
                dve.tensor_copy(row(logits, t), p_l).then_inc(S["l_sb"], 1)

            def step(t):
                ok = lambda u: not isinstance(t, int) or 0 <= u < NT
                if ok(t - 2):
                    norm_two(t - 2)
                if ok(t - 3):
                    keep_logits(t - 3)
                if ok(t + 1):
                    score_max(t + 1)
                if ok(t - 2):
                    turned_x2(t - 2)
                if ok(t + 3):
                    norm_in(t + 3)
                if ok(t + 1):
                    score_sub(t + 1)
                if ok(t - 1):
                    residual(t - 1)
                if ok(t):
                    normalise(t)

            norm_in(0)
            norm_in(1)
            score_max(0)
            score_sub(0)
            norm_in(2)
            for t in range(3):
                step(t)
            each(dve, 3, NT - 3, step)
            for t in range(NT - 3, NT + 3):
                step(t)

            n_route = [2]

            def then(instruction):
                n_route[0] += 1
                instruction.then_inc(S["route"], 1)
                dve.wait_ge(S["route"], n_route[0])

            bc = lambda ap: ap.unsqueeze(2).to_broadcast([P, NT, E])
            dve.wait_ge(S["l_sb"], NT)
            dve.wait_ge(S["route"], 2)
            then(dve.tensor_copy(iota_e[:], iota_i[:]))
            then(dve.tensor_copy(tile_f[:], tile_i[:]))
            for k in range(TOP):
                lg = (logits, lg2)[k]
                then(dve.tensor_reduce(top[:, k, :], lg[:], AX_X, ALU.max))
                then(tt(rt[:], lg[:], bc(top[:, k, :]), ALU.is_equal))
                then(stt(rt[:], iota_e[:], -FAR, rt[:], ALU.add, ALU.mult))
                then(dve.tensor_reduce(pick[:, k, :], rt[:], AX_X, ALU.min))
                then(stt(hot[:, k, :, :], iota_e[:], -FAR, bc(pick[:, k, :]), ALU.add, ALU.is_equal))
                if k == 0:
                    then(stt(lg2[:], hot[:, 0, :, :], -1e30, logits[:], ALU.mult, ALU.add))
            tt(wexp[:, 0, :], top[:, 1, :], top[:, 0, :], ALU.subtract).then_inc(S["share_in"], 1)
            tt(chosen[:], hot[:, 0, :, :], hot[:, 1, :, :], ALU.add).then_inc(S["chosen_set"], 1)

            def rows_lo(i):
                dve.wait_ge(S["xT_hi"], i + 1)
                tt(xTl[:], p_x, xTh[:].bitcast(F32), ALU.subtract).then_inc(S["xT_lo"], 1)

            def hidden_lo(i):
                for n in range(2):
                    dve.wait_ge(S["hT_hi"], 2 * i + n + 1)
                    part = slice(n * (FC // 2), (n + 1) * (FC // 2))
                    tt(hTl[:, part, :], p_hT[:, n, :, :], hTh[:, part, :].bitcast(F32), ALU.subtract
                       ).then_inc(S["hT_lo"], 1)

            def add_b1(i, s):
                for n in range(2):
                    dve.wait_ge(S["h_ps"], 2 * i + n + 1)
                    tt(hid[:, n, :], p_h[:, n, :],
                       b1bc[:, bass.ds(s, 1), n * (F // 2):(n + 1) * (F // 2)].rearrange("p o f -> p (o f)"),
                       ALU.add).then_inc(S["h_add"], 1)

            def result(i, s, kind):
                dve.wait_ge(S["y_ps"], i + 1)
                tt(ysum[:], p_y[:, 0:D], row(b2bc, s), ALU.add).then_inc(S["y_mid"], 1)
                dve.wait_ge(S["y_mid"], i + 1)
                if kind == "routed":
                    if not isinstance(i, int) or i > R0:
                        dve.wait_ge(S["y_stored"], 16 * (i - R0))
                tt(yrow[:], p_y[:, D:2 * D], ysum[:], ALU.add).then_inc(S["y_sum"], 1)
                if kind != "routed":
                    t = i if kind == "early" else i - NR
                    dve.wait_ge(S["y_sum"], i + 1)
                    if isinstance(t, int) and t == NT - 1:
                        dve.wait_ge(S["out_ready"], NT)
                    stt(row(xres, t), yrow[:], tgate[:, 1:2], row(xres, t), ALU.mult, ALU.add
                        ).then_inc(S["y_done"], 1)

            def phase_at(i):
                if isinstance(i, int) and i < R0:
                    return 0
                if isinstance(i, int) and i >= R1:
                    return (PH - 1) % 2
                return dve.value_load(phase_of[0:1, bass.ds(i, 1)], min_val=0, max_val=PH - 1) % 2

            def combine(j):
                dve.wait_ge(g_in[j], 16 * 2 * TOP)
                dve.wait_ge(S["y_done"], NA + j)
                for t in (2 * j, 2 * j + 1):
                    for k in range(TOP):
                        if k == 1:
                            dve.wait_ge(S["g_mid"], t + 1)
                        stt(xres[:, t, :], gath[:, t, k, :], share[:, k, t:t + 1], xres[:, t, :], ALU.mult, ALU.add
                            ).then_inc(S["g_mid"] if k == 0 else S["out_ready"], 1)

            def tile(i, kind, now=None, last=None, j=None):
                known = isinstance(i, int)
                if not known or i >= 1:
                    hidden_lo(i - 1)
                if not known or i < TILES:
                    add_b1(i, phase_at(i) if now is None else now)
                if not known or i < TILES - 1:
                    rows_lo(i + 1)
                if j is not None:
                    combine(j)
                if not known or i >= 1:
                    result(i - 1, phase_at(i - 1) if last is None else last, kind)

            rows_lo(0)
            tile(0, "early")

            dve.wait_ge(S["rank_ps"], 1)
            flat = lambda k: cum[:, k, :, :].rearrange("p t e -> p (t e)")
            then(dve.tensor_copy(flat(0), p_tot))
            shift, k = 1, 0
            while shift < NT:
                then(dve.tensor_copy(flat(1 - k)[:, 0:shift * E], flat(k)[:, 0:shift * E]))
                then(tt(flat(1 - k)[:, shift * E:], flat(k)[:, shift * E:], flat(k)[:, 0:(NT - shift) * E], ALU.add))
                shift, k = 2 * shift, 1 - k
            total = cum[:, k, NT - 1, :]
            then(ts(etiles[:, 0, :], total, float(P - 1), None, ALU.add))
            then(dve.tensor_copy(cnt_i[:], etiles[:, 0, :]))
            then(ts(cnt_i[:], cnt_i[:], 7, None, ALU.logical_shift_right))
            then(dve.tensor_copy(etiles[:, 0, :], cnt_i[:]))
            then(dve.tensor_copy(etiles[:, 2, :], etiles[:, 0, :]))
            shift, m = 1, 0
            while shift < E:
                then(dve.tensor_copy(etiles[:, 1 - m, 0:shift], etiles[:, m, 0:shift]))
                then(tt(etiles[:, 1 - m, shift:], etiles[:, m, shift:], etiles[:, m, 0:E - shift], ALU.add))
                shift, m = 2 * shift, 1 - m
            then(tt(etiles[:, m, :], etiles[:, m, :], etiles[:, 2, :], ALU.subtract))
            then(tt(flat(k), flat(k), p_tot, ALU.subtract))
            then(tt(place[:].rearrange("p t e -> p (t e)"), flat(k), p_rank, ALU.add))
            then(stt(place[:], etiles[:, m, :].unsqueeze(1).to_broadcast([P, NT, E]), float(P), place[:],
                     ALU.mult, ALU.add))
            for q in range(TOP):
                then(tt(rt[:], hot[:, q, :, :], place[:], ALU.mult))
                then(dve.tensor_reduce(posf[:, q, :], rt[:], AX_X, ALU.add))
            then(dve.tensor_copy(slot_y[:], posf[:]))
            then(ts(posf[:], posf[:], float(R0 * P), None, ALU.add))
            dve.tensor_copy(slot_x[:], posf[:]).then_inc(S["slots_set"], 1)
            then(dve.memset(starts[:], 0.0))
            then(ts(starts[0:1, 1:1 + E], etiles[0:1, m, :], float(R0), None, ALU.add))
            then(dve.memset(starts[0:1, 1 + E:PH], float(R1)))
            dve.tensor_copy(first_tile[:], starts[:]).then_inc(S["tables_set"], 1)
            then(tt(started[:], tile_f[:], starts[0:1, 1:PH].unsqueeze(1).to_broadcast([1, TILES, PH - 1]), ALU.is_ge))
            then(dve.tensor_reduce(phase_f[:], started[:], AX_X, ALU.add))
            dve.tensor_copy(phase_of[:], phase_f[:]).then_inc(S["tables_set"], 1)
            dve.wait_ge(S["share_exp"], 1)
            then(ts(wexp[:, 2, :], wexp[:, 1, :], 1.0, None, ALU.add))
            then(dve.reciprocal(wexp[:, 3, :], wexp[:, 2, :]))
            then(ts(share[:, 0, :], wexp[:, 3, :], tgate[:, 1:2], None, ALU.mult))
            then(tt(share[:, 1, :], share[:, 0, :], wexp[:, 1, :], ALU.mult))
            dve.wait_ge(S["tables_set"], 2)

            each(dve, 1, R0, lambda i: tile(i, "early", 0, 0))
            tile(R0, "early")
            each(dve, R0 + 1, R1 + 1, lambda i: tile(i, "routed"))
            for i in range(R1 + 1, TILES + 1):
                tile(i, "late", j=i - R1 - 1)


_INS = ['x', 'ctx_1024', 'mask_BxS2_bf0', 'g_xattn', 'g_ffn', 'L0_xattn_Wq', 'L0_xattn_bq', 'L0_xattn_Wk',
        'L0_xattn_bk', 'L0_xattn_Wv', 'L0_xattn_bv', 'L0_xattn_Wo', 'L0_xattn_bo', 'L0_ffn_gate_w', 'L0_ffn_W1',
        'L0_ffn_b1', 'L0_ffn_W2', 'L0_ffn_b2', 'L0_ffn_sW1', 'L0_ffn_sb1', 'L0_ffn_sW2', 'L0_ffn_sb2']


def kernel(**inputs):
    import numpy as np
    import concourse.bacc as bacc
    from concourse import mybir as mb
    from concourse.bass_utils import run_bass_kernel_spmd

    nc = bacc.Bacc("TRN2", target_bir_lowering=False, num_devices=1)
    arrays, args = {}, []
    for name in _INS:
        a = np.ascontiguousarray(inputs[name])
        arrays[f"in_{name}"] = a
        args.append(nc.dram_tensor(f"in_{name}", a.shape, mb.dt.from_np(a.dtype), kind="ExternalInput").ap())
    shape = inputs["x"].shape
    args.append(nc.dram_tensor("out_0", shape, mb.dt.float32, kind="ExternalOutput").ap())
    gated_cross_attention_and_moe(nc, *args)
    r = run_bass_kernel_spmd(nc, [arrays], core_ids=[0])
    return r.results[0]["out_0"]
```

```python
from contextlib import ExitStack

import concourse.bass as bass
from concourse import mybir

F32 = mybir.dt.float32
F32R = mybir.dt.float32r
BF16 = mybir.dt.bfloat16
I32 = mybir.dt.int32
U8 = mybir.dt.uint8
ALU = mybir.AluOpType
ACT = mybir.ActivationFunctionType
AX_X = mybir.AxisListType.X

P = 128
EPS = 1e-5
MASKED = -4e30
FAR = 99.0


def each(engine, first, end, body):
    if end - first == 1:
        body(first)
    elif end > first:
        with engine.Fori(first, end) as i:
            body(i)


def gated_cross_attention_and_moe(
    nc, x, ctx, mask, g_xattn, g_ffn, Wq, bq, Wk, bk, Wv, bv, Wo, bo,
    gate_w, W1, b1, W2, b2, sW1, sb1, sW2, sb2, out,
):
    B, SQ, D = x.shape
    SK = ctx.shape[1]
    H = 16
    DH = D // H
    E, _, F = W1.shape
    NT = B * SQ // P
    TB = SQ // P
    C = D // P
    FC = F // P
    HC = H // C
    CTX = B * SK
    SCALE = float(DH) ** -0.5
    HK = H * SK
    CHUNKS, NPAIR = [], 0
    for j in range(0, HK, P):
        h0, h1 = j // SK, (min(j + P, HK) - 1) // SK + 1
        CHUNKS.append((h0, h1, NPAIR, min(P, HK - j)))
        NPAIR += h1 - h0
    NCH = len(CHUNKS)
    PARTS = ((0, 4), (4, 8), (8, NCH))
    SPREAD = ((0, NCH // 2), (NCH // 2, NCH))
    assert (P, TB, C, HC * DH) == (128, 2, 2, P) and MASKED * SCALE == -1e30

    TOP = 2
    NA = NT // 2
    NB = NT - NA
    NR = (TOP * NT * P + E * (P - 1)) // P
    TILES = NA + NR + NB
    R0, R1 = NA, NA + NR
    PH = E + 2

    rows = nc.dram_tensor("ffn_rows", (TILES * P, D), F32, kind="Internal").ap()
    routed_y = nc.dram_tensor("routed_y", (NR * P, D), F32, kind="Internal").ap()
    x_v = x.rearrange("b (j p) d -> p (b j) d", p=P)
    out_v = out.rearrange("b (j p) d -> p (b j) d", p=P)
    ctx_v = ctx.rearrange("b k d -> (b k) d")
    rows_v = rows.rearrange("(t p) d -> t p d", p=P)
    y_v = routed_y.rearrange("(t p) d -> t p d", p=P)
    chunked = lambda w: w.rearrange("(c p) n -> p c n", p=P)
    W1_v = W1.rearrange("e (c p) f -> e p c f", p=P)
    W2_v = W2.rearrange("e (c p) h -> e p c h", p=P)

    with ExitStack() as stack:
        def sb(name, shape, dt=F32, where=stack):
            return where.enter_context(nc.sbuf_tensor(name, shape, dt))

        def sem(name):
            return stack.enter_context(nc.semaphore(name))

        xres = sb("xres", [P, NT, D])
        x2all = sb("x2all", [P, NT, D])
        w1h = sb("w1h", [P, 2, C, F], F32R)
        w1l = sb("w1l", [P, 2, C, F], F32R)
        w2hl = sb("w2hl", [P, 2, FC, 2 * D], F32R)
        b1bc = sb("b1bc", [P, 2, F])
        b2bc = sb("b2bc", [P, 2, D])
        stage1 = sb("stage1", [P, C, F])
        stage2 = sb("stage2", [P, FC, D])
        ident = sb("ident", [P, P])
        ones = sb("ones", [P, P])
        before = sb("before", [P, P])
        zeros = sb("zeros", [P, D])
        zeros_bf = sb("zeros_bf", [1, H * (DH + 1)], BF16)
        ones_bf = sb("ones_bf", [1, P], BF16)
        eps = sb("eps", [P, 1])
        gates = sb("gates", [P, 2])
        tgate = sb("tgate", [P, 2])
        logits = sb("logits", [P, NT, E])
        slot_y = sb("slot_y", [P, TOP, NT], I32)
        slot_x = sb("slot_x", [P, TOP, NT], I32)
        share = sb("share", [P, TOP, NT])
        phase_of = sb("phase_of", [1, TILES], I32)
        first_tile = sb("first_tile", [1, PH], I32)

        attn = ExitStack()
        a = lambda name, shape, dt=F32: sb(name, shape, dt, attn)
        wq, wk, wv, wo = (a(n, [P, C, D]) for n in ("wq", "wk", "wv", "wo"))
        bqT, bkT = a("bqT", [P, C]), a("bkT", [P, C])
        bv_bc, bo_bc = a("bv_bc", [P, D]), a("bo_bc", [P, D])
        gate_r = a("gate_r", [E, D])
        gateT = a("gateT", [P, C, E])
        headmask = a("headmask", [P, HC])
        mask_u8 = a("mask_u8", [1, CTX], U8)
        mask_bf = a("mask_bf", [1, CTX], BF16)
        NCT = (CTX + P - 1) // P
        front = a("front", [P, NCT * D])
        ctx_r = front[:].rearrange("p (t d) -> p t d", d=D)
        ctxT = a("ctxT", [P, C, CTX])
        kTh = a("kTh", [P, C, CTX], F32R)
        kTl = a("kTl", [P, C, CTX], F32R)
        kdh = a("kdh", [P, 2, C, HC, SK], F32R)
        kdl = a("kdl", [P, 2, C, HC, SK], F32R)
        vals = x2all[0:SK].rearrange("k t d -> k (t d)")[:, 0:B * H * (DH + 1)].rearrange(
            "k (b h d) -> k b h d", b=B, d=DH + 1)
        copies = a("copies", [SK, 3, SK])
        pairmask = a("pairmask", [P, NPAIR])
        spread_v = a("spread_v", [P, B, NPAIR, DH + 1])
        stats = a("stats", [P, NT, 6])
        mv = a("mv", [P, NT, 2])
        lnv = a("lnv", [P, NT])
        rstd = a("rstd", [P, NT])
        nw = a("nw", [P, 3, NT])
        xn = a("xn", [P, D])
        xnT = a("xnT", [P, C, P])
        qTh = a("qTh", [P, C, P], F32R)
        qTl = a("qTl", [P, C, P], F32R)
        smax = a("smax", [P, H])
        prob = front[:, 0:H * SK].rearrange("p (h k) -> p h k", k=SK)
        probT = a("probT", [P, NCH, P])
        rsum = a("rsum", [P, H])
        o_n = a("o_n", [P, D])
        oT = a("oT", [P, C, P])
        st2 = a("st2", [P, 6])
        mv2 = a("mv2", [P, 2])
        lnv2 = a("lnv2", [P, 1])
        r2 = a("r2", [P, 1])
        nw2 = a("nw2", [P, 4])
        x2 = a("x2", [P, D])
        x2T = a("x2T", [P, C, P])
        attn.close()

        xrow = sb("xrow", [P, D])
        xTh = sb("xTh", [P, C, P], F32R)
        xTl = sb("xTl", [P, C, P], F32R)
        hid = sb("hid", [P, 2, F // 2])
        hTh = sb("hTh", [P, FC, P], F32R)
        hTl = sb("hTl", [P, FC, P], F32R)
        yrow = sb("yrow", [P, D])
        ysum = sb("ysum", [P, D])

        gath = sb("gath", [P, NT, TOP, D])
        TE = [P, NT, E]
        iota_i = sb("iota_i", TE, I32)
        iota_e = sb("iota_e", TE)
        tile_i = sb("tile_i", [1, TILES, PH - 1], I32)
        tile_f = sb("tile_f", [1, TILES, PH - 1])
        top = sb("top", [P, TOP, NT])
        pick = sb("pick", [P, TOP, NT])
        hot = sb("hot", [P, TOP, NT, E])
        rt = sb("rt", TE)
        lg2 = sb("lg2", TE)
        chosen = sb("chosen", TE)
        cum = sb("cum", [P, 2, NT, E])
        place = sb("place", TE)
        cnt_i = sb("cnt_i", [P, E], I32)
        etiles = sb("etiles", [P, 3, E])
        starts = sb("starts", [1, PH])
        started = sb("started", [1, TILES, PH - 1])
        phase_f = sb("phase_f", [1, TILES])
        posf = sb("posf", [P, TOP, NT])
        wexp = sb("wexp", [P, 4, NT])

        ps = stack.enter_context(nc.psum_tensor("ps", [P, 8, 512], F32))
        HG = (6, 6, 4)
        p_s12 = ps[:, 0:2, 0:HG[0] * SK].rearrange("p n (h k) -> p n h k", k=SK)
        p_s3 = ps[:, 2, 0:HG[2] * SK].rearrange("p (h k) -> p h k", k=SK)
        H12 = HG[0] + HG[1]
        score_parts = ((0, 0, 6, 0, 0), (0, 6, 8, 1, 0), (1, 0, 4, 1, 2 * SK), (1, 4, 8, 2, 0))
        part_bank = (3, 4, 3)
        spread_bank = (6, 7, 3, 4, 6, 7, 6, 6)
        p_in = ps[:, 5, 0:D]
        p_l = ps[:, 5, 0:E]
        p_wo = ps[:, 6, 0:D]
        p_o = ps[:, 7, 0:H * (DH + 1)].rearrange("p (h d) -> p h d", d=DH + 1)
        k_banks, v_banks = (0, 1, 2, 5), (3, 4, 6, 7)
        p_h = ps[:, 0:2, :]
        p_hT = ps[:, 2:4, :].rearrange("p n (c q) -> p n c q", q=P)
        p_y = ps[:, 4, :]
        p_x = ps[:, 5, 0:D].rearrange("p (c q) -> p c q", q=P)
        p_rank = ps[:, 7, 0:NT * E]
        p_tot = ps[:, 7, NT * E:2 * NT * E]

        names = """consts copies_set x_in0 x_in1 ctx_in wk_in wv_in wq_in wo_in small_in zero_set rows_zeroed gate_tanh
            ctxT_ps ctxT_sb kT_ps kT_sb kT_lo gates_in v_ps v_sb mask_set gT_ps gT_sb
            ln_stats ln_mv ln_log ln_rstd ln_newton
            kd_ready xn_ready xnT_ps xnT_sb q_ps q_hi q_sb s_ps s_max p_sub p_exp pt_ps pt_sb pv_part v_spread_ps v_spread
            o_sum o_norm oT_ps oT_sb wo_ps x1_mid x1_done st2_done mv2_done ln2_log r2_done
            nw_a nw_b nw_c nw_d x2_ready x2_out x2T_ps x2T_sb l_ps l_sb
            route chosen_set rank_ps share_in share_exp tables_set slots_set scattered
            stage1_in stage2_in bias_in w1h_in w2h_in split_w1 split_w2 w_ready
            xrow_in xT_ps xT_hi xT_lo h_ps h_add h_act hT_ps hT_hi hT_lo y_ps y_mid y_sum y_done y_stored
            g_mid out_ready out_stored""".split()
        S = {n: sem(n) for n in names}
        g_in = [sem(f"g_in{j}") for j in range(NB)]
        block = stack.enter_context(nc.Block())

        def met(engine):
            engine.wait_ge(S["zero_set"], 1)

        @block.sync
        def _(sp):
            sp.dma_start(ctx_r[:, 0:NCT - 1, :],
                         ctx_v[0:(NCT - 1) * P, :].rearrange("(t p) d -> p t d", p=P)).then_inc(S["ctx_in"], 16)
            sp.dma_start(ctx_r[0:CTX - (NCT - 1) * P, NCT - 1, :],
                         ctx_v[(NCT - 1) * P:CTX, :]).then_inc(S["ctx_in"], 16)
            for dst, src, key in ((wk, Wk, "wk_in"), (wv, Wv, "wv_in")):
                sp.dma_start(dst[:], chunked(src)).then_inc(S[key], 16)
            sp.dma_start(xres[:, 0:4, :], x_v[:, 0:4, :]).then_inc(S["x_in0"], 16)
            sp.dma_start(xres[:, 4:NT, :], x_v[:, 4:NT, :]).then_inc(S["x_in1"], 16)
            for dst, src, key in ((wq, Wq, "wq_in"), (wo, Wo, "wo_in")):
                sp.dma_start(dst[:], chunked(src)).then_inc(S[key], 16)
            sp.wait_ge(S["x_in1"], 16)
            sp.wait_ge(S["zero_set"], 1)
            sp.dma_start(rows_v[R0:R1].rearrange("t p d -> p t d"),
                         zeros[:].unsqueeze(1).to_broadcast([P, NR, D])).then_inc(S["rows_zeroed"], 16)

            def keep_x2(t, row):
                sp.wait_ge(S["x2_ready"], t + 1)
                sp.dma_start(rows_v[bass.ds(row, 1)].rearrange("o p d -> (o p) d"), x2[:]).then_inc(S["x2_out"], 16)
                sp.dma_start(x2all[:, bass.ds(t, 1), :].rearrange("p o d -> p (o d)"), x2[:]).then_inc(S["x2_out"], 16)

            each(sp, 0, NA, lambda t: keep_x2(t, t))
            each(sp, NA, NT, lambda t: keep_x2(t, t + NR))
            sp.wait_ge(S["x2_out"], 32 * NT)

            def load_rows(i):
                if not isinstance(i, int) or i:
                    sp.wait_ge(S["xT_ps"], i)
                sp.dma_start(xrow[:], rows_v[bass.ds(i, 1)].rearrange("o p d -> (o p) d")).then_inc(S["xrow_in"], 16)

            sp.wait_ge(S["l_sb"], NT)
            load_rows(0)
            each(sp, 1, R0, load_rows)
            sp.wait_ge(S["scattered"], 16 * TOP * NT)
            each(sp, R0, TILES, load_rows)

            def store_out(j):
                sp.wait_ge(S["out_ready"], TOP * j + TOP)
                sp.dma_start(out_v[:, bass.ds(2 * j, 2), :], xres[:, bass.ds(2 * j, 2), :]).then_inc(S["out_stored"], 16)

            each(sp, 0, NB - 1, store_out)
            sp.wait_ge(S["y_done"], NT)
            store_out(NB - 1)
            sp.wait_ge(S["out_stored"], 16 * NB)
            sp.wait_ge(S["rows_zeroed"], 16)

        @block.gpsimd
        def _(pool):
            def load_w1(p, src):
                pool.dma_start(stage1[:], src).then_inc(S["stage1_in"], 16)

            def load_w2(p, src):
                pool.dma_start(stage2[:], src).then_inc(S["stage2_in"], 16)

            sW1_v, sW2_v = chunked(sW1), chunked(sW2)
            pool.memset(ident[:], 0.0).then_inc(S["consts"], 1)
            pool.memset(ones[:], 1.0).then_inc(S["consts"], 1)
            pool.memset(before[:], 1.0).then_inc(S["consts"], 1)
            pool.memset(headmask[:], 1.0).then_inc(S["consts"], 1)
            pool.memset(pairmask[:], 1.0).then_inc(S["consts"], 1)
            pool.wait_ge(S["consts"], 5)
            pool.affine_select(out=ident[:], in_=ident[:], compare_op=ALU.not_equal, fill=1.0, base=0,
                               pattern=[[-1, P]], channel_multiplier=1).then_inc(S["consts"], 1)
            pool.affine_select(out=before[:], in_=before[:], compare_op=ALU.is_gt, fill=0.0, base=0,
                               pattern=[[1, P]], channel_multiplier=-1).then_inc(S["consts"], 1)
            pool.affine_select(out=headmask[:], in_=headmask[:], compare_op=ALU.is_ge, fill=0.0, base=0,
                               pattern=[[-DH, HC]], channel_multiplier=1).then_inc(S["consts"], 1)
            for j, (h0, h1, pair, _) in enumerate(CHUNKS):
                m = pairmask[:, pair:pair + h1 - h0]
                ge = pool.affine_select(out=m, in_=m, compare_op=ALU.is_ge, fill=0.0, base=j * P - h0 * SK,
                                        pattern=[[-SK, h1 - h0]], channel_multiplier=1)
            ge.then_inc(S["consts"], 1)
            pool.wait_ge(S["consts"], 9)
            pool.affine_select(out=headmask[:], in_=headmask[:], compare_op=ALU.is_ge, fill=0.0, base=DH - 1,
                               pattern=[[DH, HC]], channel_multiplier=-1).then_inc(S["consts"], 1)
            for j, (h0, h1, pair, _) in enumerate(CHUNKS):
                m = pairmask[:, pair:pair + h1 - h0]
                le = pool.affine_select(out=m, in_=m, compare_op=ALU.is_ge, fill=0.0, base=(h0 + 1) * SK - 1 - j * P,
                                        pattern=[[SK, h1 - h0]], channel_multiplier=-1)
            le.then_inc(S["consts"], 1)
            pool.wait_ge(S["consts"], 11)
            pool.wait_ge(S["x_in1"], 16)
            load_w1(0, sW1_v)
            load_w2(0, sW2_v)
            pool.wait_ge(S["kT_lo"], 2 * C)

            def key_diag(b):
                if b >= 2:
                    pool.wait_ge(S["s_ps"], TB * (b - 1))
                for c in range(C):
                    for whole, part in ((kTh, kdh), (kTl, kdl)):
                        pool.tensor_tensor(
                            part[:, b % 2, c, :, :],
                            whole[:, c, b * SK:(b + 1) * SK].bitcast(F32).unsqueeze(1).to_broadcast([P, HC, SK]),
                            headmask[:].unsqueeze(2).to_broadcast([P, HC, SK]), ALU.mult
                        ).then_inc(S["kd_ready"], 1)

            def load_hi(s, first, second):
                pool.dma_start(w1h[:, bass.ds(s, 1), :, :].rearrange("p o c f -> p (o c) f"), first
                               ).then_inc(S["w1h_in"], 16)
                pool.dma_start(w2hl[:, bass.ds(s, 1), :, 0:D].rearrange("p o c f -> p (o c) f"), second
                               ).then_inc(S["w2h_in"], 16)

            def split_w1(p, s):
                pool.wait_ge(S["stage1_in"], 16 * p + 16)
                pool.wait_ge(S["w1h_in"], 16 * p + 16)
                hi = w1h[:, bass.ds(s, 1), :, :].rearrange("p o c f -> p (o c) f")
                lo = w1l[:, bass.ds(s, 1), :, :].rearrange("p o c f -> p (o c) f")
                pool.tensor_tensor(lo, stage1[:], hi.bitcast(F32), ALU.subtract).then_inc(S["split_w1"], 1)
                met(pool)
                pool.wait_ge(S["split_w1"], p + 1)

            def split_w2(p, s):
                pool.wait_ge(S["stage2_in"], 16 * p + 16)
                pool.wait_ge(S["w2h_in"], 16 * p + 16)
                both = w2hl[:, bass.ds(s, 1), :, :].rearrange("p o c f -> p (o c) f")
                pool.tensor_tensor(both[:, :, D:2 * D], stage2[:], both[:, :, 0:D].bitcast(F32),
                                   ALU.subtract).then_inc(S["split_w2"], 1)
                met(pool)
                pool.wait_ge(S["split_w2"], p + 1)

            def biases(s, first, second):
                pool.dma_start(b1bc[:, bass.ds(s, 1), :].rearrange("p o f -> p (o f)"), first).then_inc(S["bias_in"], 16)
                pool.dma_start(b2bc[:, bass.ds(s, 1), :].rearrange("p o f -> p (o f)"), second).then_inc(S["bias_in"], 16)

            def phase_ready(p):
                pool.wait_ge(S["bias_in"], 32 * p + 32)
                pool.sem_inc(S["w_ready"], 1)

            shared_b = (sb1.partition_broadcast(P), sb2.partition_broadcast(P))
            expert_b = lambda e: (b1[bass.ds(e, 1), :].rearrange("o f -> (o f)").partition_broadcast(P),
                                  b2[bass.ds(e, 1), :].rearrange("o f -> (o f)").partition_broadcast(P))
            expert_w1 = lambda e: W1_v[bass.ds(e, 1)].rearrange("o p c f -> p (o c) f")
            expert_w2 = lambda e: W2_v[bass.ds(e, 1)].rearrange("o p c f -> p (o c) f")

            pool.wait_ge(S["zero_set"], 1)
            key_diag(0)
            biases(0, *shared_b)
            load_hi(0, sW1_v, sW2_v)
            key_diag(1)
            split_w1(0, 0)
            load_w1(1, expert_w1(0))
            key_diag(2)
            split_w2(0, 0)
            load_w2(1, expert_w2(0))
            phase_ready(0)
            biases(1, *expert_b(0))
            load_hi(1, expert_w1(0), expert_w2(0))
            key_diag(3)
            split_w1(1, 1)
            load_w1(2, expert_w1(1))
            key_diag(4)
            split_w2(1, 1)
            load_w2(2, expert_w2(1))
            phase_ready(1)
            for b in range(5, B):
                key_diag(b)
            pool.wait_ge(S["l_sb"], NT)
            pool.iota(iota_i[:], pattern=[[0, NT], [1, E]], base=0, channel_multiplier=0).then_inc(S["route"], 1)
            pool.iota(tile_i[:], pattern=[[1, TILES], [0, PH - 1]], base=0, channel_multiplier=0).then_inc(S["route"], 1)

            pool.wait_ge(S["slots_set"], 1)
            pool.wait_ge(S["rows_zeroed"], 16)
            pool.wait_ge(S["x2_out"], 32 * NT)
            for t in range(NT):
                for k in range(TOP):
                    pool.indirect_dma_start(
                        out=rows, out_offset=bass.IndirectOffsetOnAxis(ap=slot_x[:, k, t:t + 1], axis=0),
                        in_=x2all[:, t, :], in_offset=None).then_inc(S["scattered"], 16)

            def phase(p, s, bias, here, ahead):
                first = pool.value_load(first_tile[0:1, bass.ds(p - 1, 1)], min_val=R0, max_val=R1)
                met(pool)
                pool.wait_ge(S["y_sum"], first)
                load_hi(s, *here)
                biases(s, *bias)
                split_w1(p, s)
                if ahead:
                    load_w1(p + 1, ahead[0])
                split_w2(p, s)
                if ahead:
                    load_w2(p + 1, ahead[1])
                phase_ready(p)

            pool.wait_ge(S["tables_set"], 1)
            with pool.Fori(2, E) as p:
                phase(p, p % 2, expert_b(p - 1), (expert_w1(p - 1), expert_w2(p - 1)), (expert_w1(p), expert_w2(p)))
            phase(E, E % 2, expert_b(E - 1), (expert_w1(E - 1), expert_w2(E - 1)), (sW1_v, sW2_v))
            phase(E + 1, (E + 1) % 2, shared_b, (sW1_v, sW2_v), None)

            pool.wait_ge(S["y_stored"], 16 * NR)
            for t in range(NT):
                for k in range(TOP):
                    pool.indirect_dma_start(
                        out=gath[:, t, k, :], out_offset=None, in_=routed_y,
                        in_offset=bass.IndirectOffsetOnAxis(ap=slot_y[:, k, t:t + 1], axis=0)
                    ).then_inc(g_in[t // 2], 16)

        @block.tensor
        def _(pe):
            mm = nc.tensor.matmul
            pe.wait_ge(S["consts"], 6)
            pe.wait_ge(S["ctx_in"], 32)
            for k in range(NCT):
                n = min(P, CTX - k * P)
                dst = ps[:, k, :]
                for c in range(C):
                    last = nc.tensor.transpose(dst[:, c * P:c * P + n], ctx_r[0:n, k, c * P:(c + 1) * P],
                                               ident[0:n, 0:n])
                last.then_inc(S["ctxT_ps"], 1)
            pe.wait_ge(S["wk_in"], 16)
            pe.wait_ge(S["ctxT_sb"], NCT)
            HALF = CTX // 2
            for co in range(C):
                for n in range(2):
                    for ci in range(C):
                        last = mm(ps[:, k_banks[2 * co + n], 0:HALF], wk[:, ci, co * P:(co + 1) * P],
                                  ctxT[:, ci, n * HALF:(n + 1) * HALF], start=ci == 0, stop=ci == C - 1)
                    last.then_inc(S["kT_ps"], 1)
            pe.wait_ge(S["wv_in"], 16)
            for b in range(B):
                dst = ps[0:SK, v_banks[b // 2], :]
                for ci in range(C):
                    last = mm(dst[:, (b % 2) * D:(b % 2 + 1) * D], ctxT[:, ci, b * SK:(b + 1) * SK], wv[:, ci, :],
                              start=ci == 0, stop=ci == C - 1)
                if b % 2:
                    last.then_inc(S["v_ps"], 1)
            pe.wait_ge(S["small_in"], 16 * 6)
            pe.wait_ge(S["v_sb"], B // 2)
            for c in range(C):
                last = nc.tensor.transpose(ps[:, 7, c * E:(c + 1) * E], gate_r[:, c * P:(c + 1) * P],
                                           ident[0:E, 0:E])
            last.then_inc(S["gT_ps"], 1)
            pe.wait_ge(S["gT_sb"], 1)

            def norm_in(t):
                pe.wait_ge(S["xn_ready"], t + 1)
                for c in range(C):
                    last = nc.tensor.transpose(p_in[:, c * P:(c + 1) * P], xn[:, c * P:(c + 1) * P], ident[:])
                last.then_inc(S["xnT_ps"], 1)

            def queries(t):
                pe.wait_ge(S["xnT_sb"], t + 1)
                for co in range(C):
                    for ci in range(C):
                        last = mm(p_in[:, co * P:(co + 1) * P], wq[:, ci, co * P:(co + 1) * P], xnT[:, ci, :],
                                  start=ci == 0, stop=ci == C - 1)
                last.then_inc(S["q_ps"], 1)

            def scores(t):
                if not isinstance(t, int) or t >= 1:
                    pe.wait_ge(S["p_sub"], t)
                pe.wait_ge(S["q_sb"], t + 1)
                b = t // TB
                pe.wait_ge(S["kd_ready"], 2 * C * (b + 1))
                for c, h0, h1, n, col in score_parts:
                    dst = ps[:, n, col:col + (h1 - h0) * SK]
                    for q, keys in ((qTh, kdl), (qTh, kdh), (qTl, kdh)):
                        mm(dst, q[:, c, :], keys[:, bass.ds(b % 2, 1), c, h0:h1, :].rearrange("p o h k -> p (o h k)"),
                           start=keys is kdl, stop=False)
                    masked = mask_bf[0:1, bass.ds(b * SK, SK)].unsqueeze(1).to_broadcast([1, h1 - h0, SK])
                    last = mm(dst, ones_bf[0:1, :], masked, start=False, stop=True)
                last.then_inc(S["s_ps"], 1)

            def spread(q):
                pair, (j0, j1) = q // 2, SPREAD[q % 2]
                first = CHUNKS[j0][2]
                wide = CHUNKS[j1 - 1][2] + CHUNKS[j1 - 1][1] - CHUNKS[j1 - 1][0] - first
                out_v = ps[:, spread_bank[q], 0:2 * wide * (DH + 1)].rearrange("p (b n d) -> p b n d", b=2, d=DH + 1)
                for j in range(j0, j1):
                    h0, h1, at, n = CHUNKS[j]
                    key0 = j * P % SK
                    last = mm(out_v[0:n, :, at - first:at - first + h1 - h0, :],
                              copies[:].rearrange("k o q -> k (o q)")[:, key0:key0 + n],
                              vals[:, 2 * pair:2 * pair + 2, h0:h1, :], start=True, stop=True)
                last.then_inc(S["v_spread_ps"], 1)

            def turn_probs(t, g):
                if g == 0:
                    pe.wait_ge(S["p_exp"], t + 1)
                    if not isinstance(t, int) or t >= 1:
                        pe.wait_ge(S["pt_sb"], 3 * t)
                if g == 2:
                    pe.wait_ge(S["pt_sb"], 3 * t + 1)
                j0, j1 = PARTS[g]
                for j in range(j0, j1):
                    n = CHUNKS[j][3]
                    last = nc.tensor.transpose(ps[0:n, part_bank[g], (j - j0) * P:(j - j0 + 1) * P],
                                               front[:, j * P:j * P + n], ident[:])
                last.then_inc(S["pt_ps"], 1)

            def attend(t, g):
                if g == 0:
                    if not isinstance(t, int) or t >= 1:
                        pe.wait_ge(S["o_norm"], t)
                    mm(p_o, zeros_bf[:, 0:P], zeros_bf[:].rearrange("o (h d) -> o h d", d=DH + 1),
                       start=True, stop=False)
                pe.wait_ge(S["pt_sb"], 3 * t + g + 1)
                for j in range(*PARTS[g]):
                    h0, h1, at, n = CHUNKS[j]
                    last = mm(p_o[:, h0:h1, :], probT[0:n, j, :],
                              spread_v[0:n, bass.ds(t // TB, 1), at:at + h1 - h0, :].rearrange("k o n d -> k (o n) d"),
                              start=False, stop=j == NCH - 1)
                last.then_inc(S["pv_part"], 1)

            def turn_heads(t):
                pe.wait_ge(S["o_norm"], t + 1)
                if not isinstance(t, int) or t >= 1:
                    pe.wait_ge(S["x1_mid"], t)
                for c in range(C):
                    last = nc.tensor.transpose(p_wo[:, c * P:(c + 1) * P], o_n[:, c * P:(c + 1) * P], ident[:])
                last.then_inc(S["oT_ps"], 1)

            def project(t):
                pe.wait_ge(S["oT_sb"], t + 1)
                for c in range(C):
                    last = mm(p_wo, oT[:, c, :], wo[:, c, :], start=c == 0, stop=c == C - 1)
                last.then_inc(S["wo_ps"], 1)

            def turn_x2(t):
                pe.wait_ge(S["x2_ready"], t + 1)
                for c in range(C):
                    last = nc.tensor.transpose(p_in[:, c * P:(c + 1) * P], x2[:, c * P:(c + 1) * P], ident[:])
                last.then_inc(S["x2T_ps"], 1)

            def route_logits(t):
                pe.wait_ge(S["x2T_sb"], t + 1)
                for c in range(C):
                    last = mm(p_l, x2T[:, c, :], gateT[:, c, :], start=c == 0, stop=c == C - 1)
                last.then_inc(S["l_ps"], 1)

            def step(t):
                known = isinstance(t, int)
                ok = lambda u: not known or 0 <= u < NT
                if ok(t - 3):
                    pe.wait_ge(S["q_sb"], t + 2 if ok(t + 1) else NT)
                    route_logits(t - 3)
                if known and t == 0:
                    pe.wait_ge(S["v_spread"], 2)
                    spread(4)
                    spread(5)
                if known and t == 1:
                    spread(6)
                if known and t == 2:
                    pe.wait_ge(S["x1_mid"], 1)
                    spread(7)
                if ok(t + 1):
                    scores(t + 1)
                if ok(t - 2):
                    if ok(t - 3):
                        pe.wait_ge(S["l_sb"], t - 2)
                    turn_x2(t - 2)
                if known and t in (0, 1, 2):
                    pe.wait_ge(S["v_spread"], (6, 7, 8)[t])
                if ok(t):
                    turn_probs(t, 0)
                    turn_probs(t, 1)
                if ok(t - 1):
                    turn_heads(t - 1)
                if ok(t):
                    turn_probs(t, 2)
                if ok(t + 2):
                    if ok(t - 2):
                        pe.wait_ge(S["x2T_sb"], t - 1)
                    norm_in(t + 2)
                if ok(t):
                    attend(t, 0)
                if ok(t + 2):
                    queries(t + 2)
                if ok(t - 1):
                    project(t - 1)
                if ok(t):
                    attend(t, 1)
                    attend(t, 2)

            pe.wait_ge(S["kT_lo"], 2 * C)
            norm_in(0)
            pe.wait_ge(S["wq_in"], 16)
            pe.wait_ge(S["wo_in"], 16)
            queries(0)
            pe.wait_ge(S["q_sb"], 1)
            norm_in(1)
            pe.wait_ge(S["mask_set"], 2)
            scores(0)
            queries(1)
            pe.wait_ge(S["copies_set"], 1)
            for q in range(4):
                spread(q)
            step(0)
            step(1)
            step(2)
            each(pe, 3, NT - 2, step)
            for t in range(NT - 2, NT + 3):
                step(t)

            def ranks():
                pe.wait_ge(S["chosen_set"], 1)
                moving = chosen[:].rearrange("p t e -> p (t e)")
                mm(p_rank, before[:], moving, start=True, stop=True)
                mm(p_tot, ones[:], moving, start=True, stop=True).then_inc(S["rank_ps"], 1)

            def turn_rows(i):
                pe.wait_ge(S["xrow_in"], 16 * i + 16)
                for c in range(C):
                    last = nc.tensor.transpose(p_x[:, c, :], xrow[:, c * P:(c + 1) * P], ident[:])
                last.then_inc(S["xT_ps"], 1)

            def turn_hidden(i):
                for n in range(2):
                    pe.wait_ge(S["h_act"], 2 * i + n + 1)
                    for c in range(FC // 2):
                        last = nc.tensor.transpose(p_hT[:, n, c, :], hid[:, n, c * P:(c + 1) * P], ident[:])
                    last.then_inc(S["hT_ps"], 1)

            def up(i, p, s):
                pe.wait_ge(S["w_ready"], p + 1)
                pe.wait_ge(S["xT_lo"], i + 1)
                for n in range(2):
                    if not isinstance(i, int) or i >= 1:
                        pe.wait_ge(S["h_add"], 2 * i - 1 + n)
                    part = lambda w, c: w[:, bass.ds(s, 1), c, n * (F // 2):(n + 1) * (F // 2)].rearrange(
                        "p o f -> p (o f)")
                    for c in range(C):
                        mm(p_h[:, n, :], xTh[:, c, :], part(w1l, c), start=c == 0, stop=False)
                        mm(p_h[:, n, :], xTh[:, c, :], part(w1h, c), start=False, stop=False)
                        last = mm(p_h[:, n, :], xTl[:, c, :], part(w1h, c), start=False, stop=c == C - 1)
                    last.then_inc(S["h_ps"], 1)

            def down(i, s):
                pe.wait_ge(S["hT_lo"], 2 * i + 2)
                if not isinstance(i, int) or i >= 1:
                    pe.wait_ge(S["y_sum"], i)
                for c in range(FC):
                    part = lambda n: w2hl[:, bass.ds(s, 1), c, 0:n].rearrange("p o f -> p (o f)")
                    mm(p_y, hTh[:, c, :], part(2 * D), start=c == 0, stop=False)
                    last = mm(p_y[:, 0:D], hTl[:, c, :], part(D), start=False, stop=c == FC - 1)
                last.then_inc(S["y_ps"], 1)

            def phase_at(i):
                if isinstance(i, int) and i < R0:
                    return 0, 0
                if isinstance(i, int) and i >= R1:
                    return PH - 1, (PH - 1) % 2
                p = pe.value_load(phase_of[0:1, bass.ds(i, 1)], min_val=0, max_val=PH - 1)
                return p, p % 2

            def tile(i, now=None, last=None):
                known = isinstance(i, int)
                if not known or i >= 1:
                    turn_hidden(i - 1)
                if not known or i < TILES:
                    up(i, *(now or phase_at(i)))
                if not known or i < TILES - 1:
                    turn_rows(i + 1)
                if not known or i >= 1:
                    down(i - 1, (last or phase_at(i - 1))[1])

            pe.wait_ge(S["l_sb"], NT)
            turn_rows(0)
            tile(0)
            ranks()
            tile(1, (0, 0), (0, 0))
            each(pe, 2, R0, lambda i: tile(i, (0, 0), (0, 0)))
            pe.wait_ge(S["tables_set"], 2)
            tile(R0)
            each(pe, R0 + 1, TILES - 1, tile)
            tile(TILES - 1)
            tile(TILES)

        @block.scalar
        def _(act):
            act.dma_start(gates[:, 0:1], g_xattn.partition_broadcast(P)).then_inc(S["gates_in"], 16)
            act.dma_start(gates[:, 1:2], g_ffn.partition_broadcast(P)).then_inc(S["gates_in"], 16)
            for dst, src in ((bkT, bk), (bqT, bq)):
                act.dma_start(dst[:], src.rearrange("(c p) -> p c", p=P), allow_slow_non_contiguous=True
                              ).then_inc(S["small_in"], 16)
            act.dma_start(mask_u8[:], mask.rearrange("b k -> (b k)").unsqueeze(0)).then_inc(S["small_in"], 16)
            act.dma_start(gate_r[:], gate_w).then_inc(S["small_in"], 16)
            act.dma_start(bv_bc[:], bv.partition_broadcast(P)).then_inc(S["small_in"], 16)
            act.dma_start(bo_bc[:], bo.partition_broadcast(P)).then_inc(S["small_in"], 16)
            act.wait_ge(S["gates_in"], 32)
            act.activation(tgate[:], gates[:], ACT.Tanh).then_inc(S["gate_tanh"], 1)
            act.preload_act_table_set("natural_log_exp_and_others")
            for k in range(NCT):
                n = min(P, CTX - k * P)
                src = ps[:, k, :]
                act.wait_ge(S["ctxT_ps"], k + 1)
                act.activation(ctxT[:, :, k * P:k * P + n],
                               src[:, 0:C * P].rearrange("p (c q) -> p c q", q=P)[:, :, 0:n],
                               ACT.Copy).then_inc(S["ctxT_sb"], 1)
            act.wait_ge(S["small_in"], 16 * 6)
            for co in range(C):
                for n in range(2):
                    act.wait_ge(S["kT_ps"], 2 * co + n + 1)
                    act.activation(kTh[:, co, n * CTX // 2:(n + 1) * CTX // 2], ps[:, k_banks[2 * co + n], 0:CTX // 2],
                                   ACT.Identity, bias=bkT[:, co:co + 1]).then_inc(S["kT_sb"], 1)
            act.wait_ge(S["ln_mv"], NT)
            act.activation(lnv[:], mv[:, :, 1], ACT.Ln, bias=eps[:, 0:1]).then_inc(S["ln_log"], 1)
            act.wait_ge(S["ln_log"], 1)
            act.activation(rstd[:], lnv[:], ACT.Exp, scale=-0.5).then_inc(S["ln_rstd"], 1)

            def norm_in(t):
                act.wait_ge(S["xnT_ps"], t + 1)
                act.activation(xnT[:].rearrange("p c q -> p (c q)"), p_in, ACT.Copy).then_inc(S["xnT_sb"], 1)

            def queries(t):
                act.wait_ge(S["q_ps"], t + 1)
                if not isinstance(t, int) or t >= 1:
                    act.wait_ge(S["s_ps"], t)
                for c in range(C):
                    last = act.activation(qTh[:, c, :], p_in[:, c * P:(c + 1) * P], ACT.Identity, bias=bqT[:, c:c + 1])
                last.then_inc(S["q_hi"], 1)

            def exponent(t):
                act.wait_ge(S["p_sub"], t + 1)
                act.activation(front[:, 0:H * SK], front[:, 0:H * SK], ACT.Exp, scale=SCALE).then_inc(S["p_exp"], 1)

            def turned_probs(t, g):
                act.wait_ge(S["pt_ps"], 3 * t + g + 1)
                if not isinstance(t, int) or t >= 1:
                    act.wait_ge(S["pv_part"], 3 * t + g - 2)
                j0, j1 = PARTS[g]
                act.activation(probT[:, j0:j1, :], ps[:, part_bank[g], 0:(j1 - j0) * P].rearrange(
                    "p (j q) -> p j q", q=P), ACT.Copy).then_inc(S["pt_sb"], 1)

            def turned_heads(t):
                act.wait_ge(S["oT_ps"], t + 1)
                act.activation(oT[:].rearrange("p c q -> p (c q)"), p_wo, ACT.Copy).then_inc(S["oT_sb"], 1)

            def deviation(t):
                act.wait_ge(S["mv2_done"], t + 1)
                act.activation(lnv2[:], mv2[:, 1:2], ACT.Ln, bias=eps[:, 0:1]).then_inc(S["ln2_log"], 1)
                act.wait_ge(S["ln2_log"], t + 1)
                act.activation(r2[:], lnv2[:], ACT.Exp, scale=-0.5).then_inc(S["r2_done"], 1)

            def step(t):
                ok = lambda u: not isinstance(t, int) or 0 <= u < NT
                if ok(t):
                    turned_probs(t, 0)
                    turned_probs(t, 1)
                if ok(t - 1):
                    turned_heads(t - 1)
                if ok(t + 2):
                    norm_in(t + 2)
                if ok(t):
                    turned_probs(t, 2)
                if ok(t + 2):
                    queries(t + 2)
                if ok(t + 1):
                    exponent(t + 1)
                if ok(t - 1):
                    deviation(t - 1)

            norm_in(0)
            queries(0)
            norm_in(1)
            queries(1)
            exponent(0)
            step(0)
            step(1)
            each(act, 2, NT - 2, step)
            for t in range(NT - 2, NT + 1):
                step(t)

            def rows_hi(i):
                act.wait_ge(S["xT_ps"], i + 1)
                act.activation(xTh[:], p_x, ACT.Copy).then_inc(S["xT_hi"], 1)

            def hidden_hi(i):
                for n in range(2):
                    act.wait_ge(S["hT_ps"], 2 * i + n + 1)
                    act.activation(hTh[:, n * (FC // 2):(n + 1) * (FC // 2), :], p_hT[:, n, :, :],
                                   ACT.Copy).then_inc(S["hT_hi"], 1)

            def gelu(i):
                for n in range(2):
                    act.wait_ge(S["h_add"], 2 * i + n + 1)
                    act.activation(hid[:, n, :], hid[:, n, :], ACT.Gelu).then_inc(S["h_act"], 1)

            def store_y(i):
                act.wait_ge(S["y_sum"], i + 1)
                act.dma_start(y_v[bass.ds(i - R0, 1)].rearrange("o p d -> (o p) d"), yrow[:]).then_inc(S["y_stored"], 16)

            def tile(i, store=False):
                known = isinstance(i, int)
                if not known or i >= 1:
                    hidden_hi(i - 1)
                if store:
                    store_y(i - 2)
                if not known or i < TILES:
                    gelu(i)
                if not known or i < TILES - 1:
                    rows_hi(i + 1)

            rows_hi(0)
            act.wait_ge(S["share_in"], 1)
            act.activation(wexp[:, 1, :], wexp[:, 0, :], ACT.Exp).then_inc(S["share_exp"], 1)
            tile(0)
            each(act, 1, R0 + 2, tile)
            each(act, R0 + 2, R1 + 2, lambda i: tile(i, True))
            each(act, R1 + 2, TILES - 1, tile)
            tile(TILES - 1)
            tile(TILES)

        @block.vector
        def _(dve):
            tt, ts, stt = dve.tensor_tensor, dve.tensor_scalar, dve.scalar_tensor_tensor
            dve.memset(zeros[:], 0.0).then_inc(S["zero_set"], 1)
            dve.memset(eps[:], EPS)
            dve.memset(vals[:], 1.0).then_inc(S["mask_set"], 1)
            dve.memset(ones_bf[:], 1.0)
            dve.memset(zeros_bf[:], 0.0)
            dve.wait_ge(S["consts"], 6)
            dve.tensor_copy(copies[:], ident[0:SK, 0:SK].unsqueeze(1).to_broadcast([SK, 3, SK])
                            ).then_inc(S["copies_set"], 1)
            dve.wait_ge(S["small_in"], 16 * 6)
            ts(mask_bf[:], mask_u8[:], MASKED, None, ALU.mult).then_inc(S["mask_set"], 1)
            for t in range(NT):
                if t == 0:
                    dve.wait_ge(S["x_in0"], 16)
                if t == 4:
                    dve.wait_ge(S["x_in1"], 16)
                dve.bn_stats(stats[:, t, :], xres[:, t, :]).then_inc(S["ln_stats"], 1)
            for t in range(NT):
                dve.wait_ge(S["ln_stats"], t + 1)
                dve.bn_aggr(mv[:, t, :], stats[:, t, :]).then_inc(S["ln_mv"], 1)
            for n in range(2 * C):
                dve.wait_ge(S["kT_sb"], n + 1)
                part = slice(n % 2 * CTX // 2, (n % 2 + 1) * CTX // 2)
                stt(kTl[:, n // 2, part], ps[:, k_banks[n], 0:CTX // 2], bkT[:, n // 2:n // 2 + 1],
                    kTh[:, n // 2, part].bitcast(F32), ALU.add, ALU.subtract).then_inc(S["kT_lo"], 1)
            dve.wait_ge(S["mask_set"], 1)
            for n in range(B // 2):
                src = ps[0:SK, v_banks[n], :]
                dve.wait_ge(S["v_ps"], n + 1)
                tt(vals[:, 2 * n:2 * n + 2, :, 0:DH],
                   src.rearrange("k (b h d) -> k b h d", b=2, d=DH),
                   bv_bc[0:SK, :].rearrange("k (h d) -> k h d", d=DH).unsqueeze(1).to_broadcast([SK, 2, H, DH]),
                   ALU.add).then_inc(S["v_sb"], 1)
            dve.wait_ge(S["gT_ps"], 1)
            dve.tensor_copy(gateT[:], ps[:, 7, 0:C * E].rearrange("p (c e) -> p c e", e=E)).then_inc(S["gT_sb"], 1)

            dve.wait_ge(S["ln_rstd"], 1)
            tt(nw[:, 0, :], rstd[:], rstd[:], ALU.mult).then_inc(S["ln_newton"], 1)
            dve.wait_ge(S["ln_newton"], 1)
            stt(nw[:, 1, :], mv[:, :, 1], EPS, nw[:, 0, :], ALU.add, ALU.mult).then_inc(S["ln_newton"], 1)
            dve.wait_ge(S["ln_newton"], 2)
            ts(nw[:, 2, :], nw[:, 1, :], -0.5, 1.5, ALU.mult, ALU.add).then_inc(S["ln_newton"], 1)
            dve.wait_ge(S["ln_newton"], 3)
            tt(rstd[:], rstd[:], nw[:, 2, :], ALU.mult).then_inc(S["ln_newton"], 1)
            dve.wait_ge(S["ln_newton"], 4)
            dve.wait_ge(S["gate_tanh"], 1)

            def col(ap, t):
                return ap[:, bass.ds(t, 1)]

            def row(ap, t):
                return ap[:, bass.ds(t, 1), :].rearrange("p o d -> p (o d)")

            def norm_in(t):
                if not isinstance(t, int) or t >= 1:
                    dve.wait_ge(S["xnT_ps"], t)
                ts(xn[:], row(xres, t), row(mv, t)[:, 0:1], col(rstd, t), ALU.subtract, ALU.mult
                   ).then_inc(S["xn_ready"], 1)

            def queries_lo(t):
                dve.wait_ge(S["q_hi"], t + 1)
                for c in range(C):
                    last = stt(qTl[:, c, :], p_in[:, c * P:(c + 1) * P], bqT[:, c:c + 1], qTh[:, c, :].bitcast(F32),
                               ALU.add, ALU.subtract)
                last.then_inc(S["q_sb"], 1)

            def score_max(t):
                dve.wait_ge(S["s_ps"], t + 1)
                dve.tensor_reduce(smax[:, 0:H12].rearrange("p (n h) -> p n h", n=2), p_s12, AX_X, ALU.max)
                dve.tensor_reduce(smax[:, H12:H], p_s3, AX_X, ALU.max).then_inc(S["s_max"], 1)

            def score_sub(t):
                if not isinstance(t, int) or t >= 1:
                    dve.wait_ge(S["pt_ps"], 3 * t)
                dve.wait_ge(S["s_max"], t + 1)
                tt(prob[:, 0:H12, :].rearrange("p (n h) k -> p n h k", n=2), p_s12,
                   smax[:, 0:H12].rearrange("p (n h) -> p n h", n=2).unsqueeze(3).to_broadcast([P, 2, HG[0], SK]),
                   ALU.subtract)
                tt(prob[:, H12:H, :], p_s3, smax[:, H12:H].unsqueeze(2).to_broadcast([P, HG[2], SK]),
                   ALU.subtract).then_inc(S["p_sub"], 1)

            def normalise(t):
                dve.wait_ge(S["pv_part"], 3 * t + 3)
                dve.reciprocal(rsum[:], p_o[:, :, DH]).then_inc(S["o_sum"], 1)
                if not isinstance(t, int) or t >= 1:
                    dve.wait_ge(S["oT_ps"], t)
                dve.wait_ge(S["o_sum"], t + 1)
                tt(o_n[:].rearrange("p (h d) -> p h d", d=DH), p_o[:, :, 0:DH],
                   rsum[:].unsqueeze(2).to_broadcast([P, H, DH]), ALU.mult).then_inc(S["o_norm"], 1)

            def spread_out(q):
                dve.wait_ge(S["v_spread_ps"], q + 1)
                pair, (j0, j1) = q // 2, SPREAD[q % 2]
                first = CHUNKS[j0][2]
                wide = CHUNKS[j1 - 1][2] + CHUNKS[j1 - 1][1] - CHUNKS[j1 - 1][0] - first
                full = wide if CHUNKS[j1 - 1][3] == P else CHUNKS[j1 - 1][2] - first
                src = ps[:, spread_bank[q], 0:2 * wide * (DH + 1)].rearrange("p (b n d) -> p b n d", b=2, d=DH + 1)
                for n, a0, a1 in ((P, 0, full), (CHUNKS[-1][3], full, wide)):
                    if a0 < a1:
                        last = tt(spread_v[0:n, 2 * pair:2 * pair + 2, first + a0:first + a1, :], src[0:n, :, a0:a1, :],
                                  pairmask[0:n, first + a0:first + a1].unsqueeze(1).unsqueeze(3).to_broadcast(
                                      [n, 2, a1 - a0, DH + 1]), ALU.mult)
                last.then_inc(S["v_spread"], 1)

            def residual(t):
                dve.wait_ge(S["wo_ps"], t + 1)
                stt(row(xres, t), p_wo, tgate[:, 0:1], row(xres, t), ALU.mult, ALU.add).then_inc(S["x1_mid"], 1)
                dve.wait_ge(S["x1_mid"], t + 1)
                stt(row(xres, t), bo_bc[:], tgate[:, 0:1], row(xres, t), ALU.mult, ALU.add).then_inc(S["x1_done"], 1)
                met(dve)
                dve.wait_ge(S["x1_done"], t + 1)
                dve.bn_stats(st2[:], row(xres, t)).then_inc(S["st2_done"], 1)
                met(dve)
                dve.wait_ge(S["st2_done"], t + 1)
                dve.bn_aggr(mv2[:], st2[:]).then_inc(S["mv2_done"], 1)

            def norm_two(t):
                dve.wait_ge(S["r2_done"], t + 1)
                tt(nw2[:, 0:1], r2[:], r2[:], ALU.mult).then_inc(S["nw_a"], 1)
                dve.wait_ge(S["nw_a"], t + 1)
                stt(nw2[:, 1:2], mv2[:, 1:2], EPS, nw2[:, 0:1], ALU.add, ALU.mult).then_inc(S["nw_b"], 1)
                dve.wait_ge(S["nw_b"], t + 1)
                ts(nw2[:, 2:3], nw2[:, 1:2], -0.5, 1.5, ALU.mult, ALU.add).then_inc(S["nw_c"], 1)
                dve.wait_ge(S["nw_c"], t + 1)
                tt(nw2[:, 3:4], r2[:], nw2[:, 2:3], ALU.mult).then_inc(S["nw_d"], 1)
                dve.wait_ge(S["nw_d"], t + 1)
                if not isinstance(t, int) or t >= 1:
                    dve.wait_ge(S["x2_out"], 32 * t)
                    dve.wait_ge(S["x2T_ps"], t)
                ts(x2[:], row(xres, t), mv2[:, 0:1], nw2[:, 3:4], ALU.subtract, ALU.mult).then_inc(S["x2_ready"], 1)

            def turned_x2(t):
                dve.wait_ge(S["x2T_ps"], t + 1)
                if not isinstance(t, int) or t >= 1:
                    dve.wait_ge(S["l_ps"], t)
                dve.tensor_copy(x2T[:].rearrange("p c q -> p (c q)"), p_in).then_inc(S["x2T_sb"], 1)

            def keep_logits(t):
                dve.wait_ge(S["l_ps"], t + 1)
                dve.tensor_copy(row(logits, t), p_l).then_inc(S["l_sb"], 1)

            def step(t):
                ok = lambda u: not isinstance(t, int) or 0 <= u < NT
                if ok(t - 2):
                    norm_two(t - 2)
                if ok(t - 3):
                    keep_logits(t - 3)
                for q in {0: (4, 5), 1: (6,), 2: (7,)}.get(t, ()) if isinstance(t, int) else ():
                    spread_out(q)
                if ok(t + 1):
                    score_max(t + 1)
                if ok(t - 2):
                    turned_x2(t - 2)
                if ok(t + 1):
                    score_sub(t + 1)
                if ok(t + 2):
                    queries_lo(t + 2)
                if ok(t + 3):
                    norm_in(t + 3)
                if ok(t - 1):
                    residual(t - 1)
                if ok(t):
                    normalise(t)

            norm_in(0)
            queries_lo(0)
            norm_in(1)
            queries_lo(1)
            score_max(0)
            score_sub(0)
            norm_in(2)
            dve.wait_ge(S["consts"], 11)
            for q in range(4):
                spread_out(q)
            for t in range(3):
                step(t)
            each(dve, 3, NT - 3, step)
            for t in range(NT - 3, NT + 3):
                step(t)

            n_route = [2]

            def then(instruction):
                n_route[0] += 1
                instruction.then_inc(S["route"], 1)
                dve.wait_ge(S["route"], n_route[0])

            bc = lambda ap: ap.unsqueeze(2).to_broadcast([P, NT, E])
            dve.wait_ge(S["l_sb"], NT)
            dve.wait_ge(S["route"], 2)
            then(dve.tensor_copy(iota_e[:], iota_i[:]))
            then(dve.tensor_copy(tile_f[:], tile_i[:]))
            for k in range(TOP):
                lg = (logits, lg2)[k]
                then(dve.tensor_reduce(top[:, k, :], lg[:], AX_X, ALU.max))
                then(tt(rt[:], lg[:], bc(top[:, k, :]), ALU.is_equal))
                then(stt(rt[:], iota_e[:], -FAR, rt[:], ALU.add, ALU.mult))
                then(dve.tensor_reduce(pick[:, k, :], rt[:], AX_X, ALU.min))
                then(stt(hot[:, k, :, :], iota_e[:], -FAR, bc(pick[:, k, :]), ALU.add, ALU.is_equal))
                if k == 0:
                    then(stt(lg2[:], hot[:, 0, :, :], -1e30, logits[:], ALU.mult, ALU.add))
            tt(wexp[:, 0, :], top[:, 1, :], top[:, 0, :], ALU.subtract).then_inc(S["share_in"], 1)
            tt(chosen[:], hot[:, 0, :, :], hot[:, 1, :, :], ALU.add).then_inc(S["chosen_set"], 1)

            def rows_lo(i):
                dve.wait_ge(S["xT_hi"], i + 1)
                tt(xTl[:], p_x, xTh[:].bitcast(F32), ALU.subtract).then_inc(S["xT_lo"], 1)

            def hidden_lo(i):
                for n in range(2):
                    dve.wait_ge(S["hT_hi"], 2 * i + n + 1)
                    part = slice(n * (FC // 2), (n + 1) * (FC // 2))
                    tt(hTl[:, part, :], p_hT[:, n, :, :], hTh[:, part, :].bitcast(F32), ALU.subtract
                       ).then_inc(S["hT_lo"], 1)

            def add_b1(i, s):
                for n in range(2):
                    dve.wait_ge(S["h_ps"], 2 * i + n + 1)
                    tt(hid[:, n, :], p_h[:, n, :],
                       b1bc[:, bass.ds(s, 1), n * (F // 2):(n + 1) * (F // 2)].rearrange("p o f -> p (o f)"),
                       ALU.add).then_inc(S["h_add"], 1)

            def result(i, s, kind):
                dve.wait_ge(S["y_ps"], i + 1)
                tt(ysum[:], p_y[:, 0:D], row(b2bc, s), ALU.add).then_inc(S["y_mid"], 1)
                dve.wait_ge(S["y_mid"], i + 1)
                if kind == "routed":
                    if not isinstance(i, int) or i > R0:
                        dve.wait_ge(S["y_stored"], 16 * (i - R0))
                tt(yrow[:], p_y[:, D:2 * D], ysum[:], ALU.add).then_inc(S["y_sum"], 1)
                if kind != "routed":
                    t = i if kind == "early" else i - NR
                    dve.wait_ge(S["y_sum"], i + 1)
                    if isinstance(t, int) and t == NT - 1:
                        dve.wait_ge(S["out_ready"], NT)
                    stt(row(xres, t), yrow[:], tgate[:, 1:2], row(xres, t), ALU.mult, ALU.add
                        ).then_inc(S["y_done"], 1)

            def phase_at(i):
                if isinstance(i, int) and i < R0:
                    return 0
                if isinstance(i, int) and i >= R1:
                    return (PH - 1) % 2
                return dve.value_load(phase_of[0:1, bass.ds(i, 1)], min_val=0, max_val=PH - 1) % 2

            def combine(j):
                dve.wait_ge(g_in[j], 16 * 2 * TOP)
                dve.wait_ge(S["y_done"], NA + j)
                for t in (2 * j, 2 * j + 1):
                    for k in range(TOP):
                        if k == 1:
                            dve.wait_ge(S["g_mid"], t + 1)
                        stt(xres[:, t, :], gath[:, t, k, :], share[:, k, t:t + 1], xres[:, t, :], ALU.mult, ALU.add
                            ).then_inc(S["g_mid"] if k == 0 else S["out_ready"], 1)

            def tile(i, kind, now=None, last=None, j=None):
                known = isinstance(i, int)
                if not known or i >= 1:
                    hidden_lo(i - 1)
                if not known or i < TILES:
                    add_b1(i, phase_at(i) if now is None else now)
                if not known or i < TILES - 1:
                    rows_lo(i + 1)
                if j is not None:
                    combine(j)
                if not known or i >= 1:
                    result(i - 1, phase_at(i - 1) if last is None else last, kind)

            rows_lo(0)
            tile(0, "early")

            dve.wait_ge(S["rank_ps"], 1)
            flat = lambda k: cum[:, k, :, :].rearrange("p t e -> p (t e)")
            then(dve.tensor_copy(flat(0), p_tot))
            shift, k = 1, 0
            while shift < NT:
                then(dve.tensor_copy(flat(1 - k)[:, 0:shift * E], flat(k)[:, 0:shift * E]))
                then(tt(flat(1 - k)[:, shift * E:], flat(k)[:, shift * E:], flat(k)[:, 0:(NT - shift) * E], ALU.add))
                shift, k = 2 * shift, 1 - k
            total = cum[:, k, NT - 1, :]
            then(ts(etiles[:, 0, :], total, float(P - 1), None, ALU.add))
            then(dve.tensor_copy(cnt_i[:], etiles[:, 0, :]))
            then(ts(cnt_i[:], cnt_i[:], 7, None, ALU.logical_shift_right))
            then(ts(etiles[:, 0, :], cnt_i[:], 1.0, None, ALU.max))
            then(dve.tensor_copy(etiles[:, 2, :], etiles[:, 0, :]))
            shift, m = 1, 0
            while shift < E:
                then(dve.tensor_copy(etiles[:, 1 - m, 0:shift], etiles[:, m, 0:shift]))
                then(tt(etiles[:, 1 - m, shift:], etiles[:, m, shift:], etiles[:, m, 0:E - shift], ALU.add))
                shift, m = 2 * shift, 1 - m
            then(tt(etiles[:, m, :], etiles[:, m, :], etiles[:, 2, :], ALU.subtract))
            then(tt(flat(k), flat(k), p_tot, ALU.subtract))
            then(tt(place[:].rearrange("p t e -> p (t e)"), flat(k), p_rank, ALU.add))
            then(stt(place[:], etiles[:, m, :].unsqueeze(1).to_broadcast([P, NT, E]), float(P), place[:],
                     ALU.mult, ALU.add))
            for q in range(TOP):
                then(tt(rt[:], hot[:, q, :, :], place[:], ALU.mult))
                then(dve.tensor_reduce(posf[:, q, :], rt[:], AX_X, ALU.add))
            then(dve.tensor_copy(slot_y[:], posf[:]))
            then(ts(posf[:], posf[:], float(R0 * P), None, ALU.add))
            dve.tensor_copy(slot_x[:], posf[:]).then_inc(S["slots_set"], 1)
            then(dve.memset(starts[:], 0.0))
            then(ts(starts[0:1, 1:1 + E], etiles[0:1, m, :], float(R0), None, ALU.add))
            then(dve.memset(starts[0:1, 1 + E:PH], float(R1)))
            dve.tensor_copy(first_tile[:], starts[:]).then_inc(S["tables_set"], 1)
            then(tt(started[:], tile_f[:], starts[0:1, 1:PH].unsqueeze(1).to_broadcast([1, TILES, PH - 1]), ALU.is_ge))
            then(dve.tensor_reduce(phase_f[:], started[:], AX_X, ALU.add))
            dve.tensor_copy(phase_of[:], phase_f[:]).then_inc(S["tables_set"], 1)
            dve.wait_ge(S["share_exp"], 1)
            then(ts(wexp[:, 2, :], wexp[:, 1, :], 1.0, None, ALU.add))
            then(dve.reciprocal(wexp[:, 3, :], wexp[:, 2, :]))
            then(ts(share[:, 0, :], wexp[:, 3, :], tgate[:, 1:2], None, ALU.mult))
            then(tt(share[:, 1, :], share[:, 0, :], wexp[:, 1, :], ALU.mult))
            dve.wait_ge(S["tables_set"], 2)

            each(dve, 1, R0, lambda i: tile(i, "early", 0, 0))
            tile(R0, "early")
            tile(R0 + 1, "routed")
            each(dve, R0 + 2, R1 + 1, lambda i: tile(i, "routed"))
            for i in range(R1 + 1, TILES + 1):
                tile(i, "late", j=i - R1 - 1)


_INS = ['x', 'ctx_1024', 'mask_BxS2_bf0', 'g_xattn', 'g_ffn', 'L0_xattn_Wq', 'L0_xattn_bq', 'L0_xattn_Wk',
        'L0_xattn_bk', 'L0_xattn_Wv', 'L0_xattn_bv', 'L0_xattn_Wo', 'L0_xattn_bo', 'L0_ffn_gate_w', 'L0_ffn_W1',
        'L0_ffn_b1', 'L0_ffn_W2', 'L0_ffn_b2', 'L0_ffn_sW1', 'L0_ffn_sb1', 'L0_ffn_sW2', 'L0_ffn_sb2']


def kernel(**inputs):
    import numpy as np
    import concourse.bacc as bacc
    from concourse import mybir as mb
    from concourse.bass_utils import run_bass_kernel_spmd

    nc = bacc.Bacc("TRN2", target_bir_lowering=False, num_devices=1)
    arrays, args = {}, []
    for name in _INS:
        a = np.ascontiguousarray(inputs[name])
        arrays[f"in_{name}"] = a
        args.append(nc.dram_tensor(f"in_{name}", a.shape, mb.dt.from_np(a.dtype), kind="ExternalInput").ap())
    shape = inputs["x"].shape
    args.append(nc.dram_tensor("out_0", shape, mb.dt.float32, kind="ExternalOutput").ap())
    gated_cross_attention_and_moe(nc, *args)
    r = run_bass_kernel_spmd(nc, [arrays], core_ids=[0])
    return r.results[0]["out_0"]
```

```python
from contextlib import ExitStack

import concourse.bass as bass
from concourse import mybir

F32 = mybir.dt.float32
F32R = mybir.dt.float32r
BF16 = mybir.dt.bfloat16
I32 = mybir.dt.int32
U8 = mybir.dt.uint8
ALU = mybir.AluOpType
ACT = mybir.ActivationFunctionType
AX_X = mybir.AxisListType.X

P = 128
EPS = 1e-5
MASKED = -4e30
FAR = 99.0


def each(engine, first, end, body):
    if end - first == 1:
        body(first)
    elif end > first:
        with engine.Fori(first, end) as i:
            body(i)


def in_pairs(engine, first, end, body):
    turns = (end - first) // 2
    if turns:
        with engine.Fori(0, turns) as n:
            for u in range(2):
                body(2 * n + (first + u), (first + u) % 2)
    if (end - first) % 2:
        body(end - 1, (end - 1) % 2)


def gated_cross_attention_and_moe(
    nc, x, ctx, mask, g_xattn, g_ffn, Wq, bq, Wk, bk, Wv, bv, Wo, bo,
    gate_w, W1, b1, W2, b2, sW1, sb1, sW2, sb2, out,
):
    B, SQ, D = x.shape
    SK = ctx.shape[1]
    H = 16
    DH = D // H
    E, _, F = W1.shape
    NT = B * SQ // P
    TB = SQ // P
    C = D // P
    FC = F // P
    HC = H // C
    CTX = B * SK
    SCALE = float(DH) ** -0.5
    HK = H * SK
    CHUNKS, NPAIR = [], 0
    for j in range(0, HK, P):
        h0, h1 = j // SK, (min(j + P, HK) - 1) // SK + 1
        CHUNKS.append((h0, h1, NPAIR, min(P, HK - j)))
        NPAIR += h1 - h0
    NCH = len(CHUNKS)
    PARTS = ((0, 4), (4, 8), (8, NCH))
    FIRST = 3
    SPREAD = ((0, NCH // 2), (NCH // 2, NCH))
    assert (P, TB, C, HC * DH) == (128, 2, 2, P) and MASKED * SCALE == -1e30

    TOP = 2
    NA = NT // 2 + 1
    NB = NT - NA
    NR = (TOP * NT * P + E * (P - 1)) // P
    TILES = NA + NR + NB
    R0, R1 = NA, NA + NR
    PH = E + 2

    rows = nc.dram_tensor("routed_x", (NR * P, D), F32, kind="Internal").ap()
    routed_y = nc.dram_tensor("routed_y", (NR * P, D), F32, kind="Internal").ap()
    x_v = x.rearrange("b (j p) d -> p (b j) d", p=P)
    out_v = out.rearrange("b (j p) d -> p (b j) d", p=P)
    ctx_v = ctx.rearrange("b k d -> (b k) d")
    rows_v = rows.rearrange("(t p) d -> t p d", p=P)
    y_v = routed_y.rearrange("(t p) d -> t p d", p=P)
    chunked = lambda w: w.rearrange("(c p) n -> p c n", p=P)
    W1_v = W1.rearrange("e (c p) f -> e p c f", p=P)
    W2_v = W2.rearrange("e (c p) h -> e p c h", p=P)

    with ExitStack() as stack:
        def sb(name, shape, dt=F32, where=stack):
            return where.enter_context(nc.sbuf_tensor(name, shape, dt))

        def sem(name):
            return stack.enter_context(nc.semaphore(name))

        xres = sb("xres", [P, NT, D])
        x2 = sb("x2", [P, NT, D])
        w1h = sb("w1h", [P, 2, C, F], F32R)
        w1l = sb("w1l", [P, 2, C, F], F32R)
        w2hl = sb("w2hl", [P, 2, FC, 2 * D], F32R)
        b1bc = sb("b1bc", [P, 2, F])
        b2bc = sb("b2bc", [P, 2, D])
        stage1 = sb("stage1", [P, C, F])
        stage2 = sb("stage2", [P, FC, D])
        ident = sb("ident", [P, P])
        ones = sb("ones", [P, P], BF16)
        before = sb("before", [P, P], BF16)
        earlier = sb("earlier", [P, E, E])
        iota_i = sb("iota_i", [P, E], I32)
        iota_far = sb("iota_far", [P, E])
        zeros = sb("zeros", [P, D])
        zeros_bf = sb("zeros_bf", [1, H * (DH + 1)], BF16)
        ones_bf = sb("ones_bf", [1, P], BF16)
        eps = sb("eps", [P, 1])
        neg_eps = sb("neg_eps", [P, 1])
        one_half = sb("one_half", [P, 1])
        gates = sb("gates", [P, 2])
        tgate = sb("tgate", [P, 2])
        logits = sb("logits", [P, NT, E])
        slot = sb("slot", [P, TOP, NT], I32)
        share = sb("share", [P, TOP, NT])
        phase_of = sb("phase_of", [1, TILES], I32)
        first_tile = sb("first_tile", [1, PH], I32)
        first_half = sb("first_half", [1, PH], I32)
        xrow = sb("xrow", [P, 2, D])
        xTh = sb("xTh", [P, C, P], F32R)
        xTl = sb("xTl", [P, C, P], F32R)
        hid = sb("hid", [P, 2, F // 2])

        attn = ExitStack()
        a = lambda name, shape, dt=F32: sb(name, shape, dt, attn)
        wq, wo = (a(n, [P, C, D]) for n in ("wq", "wo"))
        bqT, bkT = a("bqT", [P, C]), a("bkT", [P, C])
        bv_bc, bo_bc = a("bv_bc", [P, D]), a("bo_bc", [P, D])
        gate_r = a("gate_r", [E, D])
        gateT = a("gateT", [P, C, E])
        headmask = a("headmask", [P, HC])
        mask_u8 = a("mask_u8", [1, CTX], U8)
        mask_bf = a("mask_bf", [1, CTX], BF16)
        NCT = (CTX + P - 1) // P
        front = a("front", [P, NCT * D])
        ctx_r = front[:].rearrange("p (t d) -> p t d", d=D)
        kTh = a("kTh", [P, C, CTX], F32R)
        kTl = a("kTl", [P, C, CTX], F32R)
        kdh = a("kdh", [P, 2, C, HC, SK], F32R)
        kdl = a("kdl", [P, 2, C, HC, SK], F32R)
        vals = x2[0:SK].rearrange("k t d -> k (t d)")[:, NT * D - B * H * (DH + 1):].rearrange(
            "k (b h d) -> k b h d", b=B, d=DH + 1)
        copies = a("copies", [SK, 3, SK])
        pairmask = a("pairmask", [P, NPAIR])
        spread_v = a("spread_v", [P, B, NPAIR, DH + 1])
        early = spread_v[:].rearrange("p b n d -> p (b n d)")
        ctxT = early[:, 0:C * CTX].rearrange("p (c n) -> p c n", c=C)
        wk, wv = (early[:, C * CTX + n * C * D:C * CTX + (n + 1) * C * D].rearrange("p (c n) -> p c n", c=C)
                  for n in range(2))
        stats = a("stats", [P, NT, 6])
        mv = a("mv", [P, NT, 2])
        lnv = a("lnv", [P, NT])
        rstd = a("rstd", [P, NT])
        nw = a("nw", [P, 3, NT])
        xn = a("xn", [P, D])
        xnT = a("xnT", [P, C, P])
        qTh = a("qTh", [P, C, P], F32R)
        qTl = a("qTl", [P, C, P], F32R)
        smax = a("smax", [P, H])
        prob = front[:, 0:H * SK].rearrange("p (h k) -> p h k", k=SK)
        probT = a("probT", [P, NCH, P])
        rsum = a("rsum", [P, H])
        o_n = a("o_n", [P, D])
        oT = a("oT", [P, C, P])
        st2 = a("st2", [P, 6])
        mv2 = a("mv2", [P, 2])
        lnv2 = a("lnv2", [P, 1])
        r2 = a("r2", [P, 1])
        nw2 = a("nw2", [P, 4])
        x2row = a("x2row", [P, D])
        x2T = a("x2T", [P, C, P])
        attn.close()

        hTh = sb("hTh", [P, FC, P], F32R)
        hTl = sb("hTl", [P, FC, P], F32R)
        yrow = sb("yrow", [P, D])
        ysum = sb("ysum", [P, D])

        gath = sb("gath", [P, NT, TOP, D])
        TE = [P, NT, E]
        tile_i = sb("tile_i", [1, TILES, PH - 1], I32)
        tile_f = sb("tile_f", [1, TILES, PH - 1])
        top = sb("top", [P, TOP, NT])
        pick = sb("pick", [P, TOP, NT])
        hot = sb("hot", [P, TOP, NT, E])
        rt = sb("rt", TE)
        lg2 = sb("lg2", TE)
        chosen = sb("chosen", [P, NT + 1, E], BF16)
        place = sb("place", TE)
        cnt_i = sb("cnt_i", [P, 2, E], I32)
        etiles = sb("etiles", [P, E])
        etri = sb("etri", [P, E, E])
        ebase = sb("ebase", [P, E])
        starts = sb("starts", [1, PH])
        started = sb("started", [1, TILES, PH - 1])
        phase_f = sb("phase_f", [1, TILES])
        onplace = sb("onplace", [P, TOP, NT, E])
        posf = sb("posf", [P, TOP, NT])
        lead = sb("lead", [P, 2, NT])
        half = sb("half", [P, 2, NT])

        ps = stack.enter_context(nc.psum_tensor("ps", [P, 8, 512], F32))
        HG = (6, 6, 4)
        p_s12 = ps[:, 0:2, 0:HG[0] * SK].rearrange("p n (h k) -> p n h k", k=SK)
        p_s3 = ps[:, 2, 0:HG[2] * SK].rearrange("p (h k) -> p h k", k=SK)
        H12 = HG[0] + HG[1]
        score_parts = ((0, 0, 6, 0, 0), (0, 6, 8, 1, 0), (1, 0, 4, 1, 2 * SK), (1, 4, 8, 2, 0))
        part_bank = (3, 4, 3)
        spread_bank = (6, 7, 3, 4, 6, 7, 6, 6)
        p_in = ps[:, 5, 0:D]
        p_l = ps[:, 5, 0:E]
        p_wo = ps[:, 6, 0:D]
        p_o = ps[:, 7, 0:H * (DH + 1)].rearrange("p (h d) -> p h d", d=DH + 1)
        k_banks, v_banks = (0, 1, 2, 7), (3, 4, 6, 7)
        p_h = ps[:, 0:2, :]
        p_hT = ps[:, 2:4, :].rearrange("p n (c q) -> p n c q", q=P)
        p_y = ps[:, 4, :]
        p_x = ps[:, 5, 0:D].rearrange("p (c q) -> p c q", q=P)
        p_place = ps[:, 7, 0:(NT + 1) * E].rearrange("p (t e) -> p t e", e=E)

        names = """consts copies_set x_in0 x_in1 ctx_in wk_in wv_in wq_in wo_in bk_in bq_in
            mask_in gate_w_in bv_in bo_in zero_set rows_zeroed gate_tanh
            ctxT_ps ctxT_sb kT_ps kT_sb kT_lo gates_in v_ps v_sb mask_set gT_ps gT_sb
            ln_stats ln_mv ln_log ln_rstd ln_newton far_set
            kd_ready xn_ready xnT_ps xnT_sb q_ps q_hi q_sb s_ps s_max p_sub p_exp pt_ps pt_sb
            pv_part v_spread_ps v_spread
            o_sum o_norm oT_ps oT_sb wo_ps x1_mid x1_done st2_done mv2_done ln2_log r2_done
            nw_a nw_b nw_c nw_d x2_ready x2_out x2T_ps x2T_sb l_ps l_sb
            route tiles_set chosen_set rank_ps share_in share_tanh tables_set slots_set scattered
            stage1_in stage2_in b1_in b2_in w1h_in w2h_in split_w1 split_w2 w1_ready w2_ready
            xT_ps xT_hi xT_lo h_ps h_add h_act hT_ps hT_hi hT_lo y_ps y_mid y_sum y_done y_stored
            g_mid out_ready out_stored""".split()
        S = {n: sem(n) for n in names}
        xrow_in = [sem(f"xrow_in{n}") for n in range(2)]
        g_in = [sem(f"g_in{j}") for j in range(NT // 2)]
        block = stack.enter_context(nc.Block())

        def met(engine):
            engine.wait_ge(S["zero_set"], 1)

        @block.sync
        def _(sp):
            sp.dma_start(ctx_r[:, 0:NCT - 1, :],
                         ctx_v[0:(NCT - 1) * P, :].rearrange("(t p) d -> p t d", p=P)).then_inc(S["ctx_in"], 16)
            sp.dma_start(ctx_r[0:CTX - (NCT - 1) * P, NCT - 1, :],
                         ctx_v[(NCT - 1) * P:CTX, :]).then_inc(S["ctx_in"], 16)
            sp.dma_start(wk[:], chunked(Wk)).then_inc(S["wk_in"], 16)
            sp.dma_start(xres[:, 0:FIRST, :], x_v[:, 0:FIRST, :]).then_inc(S["x_in0"], 16)
            for dst, src, key in ((wv, Wv, "wv_in"), (wq, Wq, "wq_in")):
                sp.dma_start(dst[:], chunked(src)).then_inc(S[key], 16)
            sp.dma_start(xres[:, FIRST:NT, :], x_v[:, FIRST:NT, :]).then_inc(S["x_in1"], 16)
            sp.dma_start(wo[:], chunked(Wo)).then_inc(S["wo_in"], 16)

            def keep_x2(t):
                sp.wait_ge(S["x2_ready"], t + 1)
                sp.dma_start(x2[:, bass.ds(t, 1), :].rearrange("p o d -> p (o d)"), x2row[:]).then_inc(S["x2_out"], 16)

            def load_rows(i, parity, kind):
                if not isinstance(i, int) or i >= 2:
                    sp.wait_ge(S["xT_ps"], i - 1)
                if kind == "routed":
                    src = rows_v[bass.ds(i - R0, 1)].rearrange("o p d -> (o p) d")
                else:
                    src = x2[:, bass.ds(i if kind == "early" else i - NR, 1), :].rearrange("p o d -> p (o d)")
                sp.dma_start(xrow[:, parity, :], src).then_inc(xrow_in[parity], 16)

            each(sp, 0, NA, keep_x2)
            sp.wait_ge(S["x2_out"], 16 * NA)
            load_rows(0, 0, "early")
            load_rows(1, 1, "early")
            sp.wait_ge(S["zero_set"], 1)
            SHARE = -(-NR // NB)
            for n in range(NB):
                keep_x2(NA + n)
                part = rows_v[n * SHARE:min((n + 1) * SHARE, NR)]
                sp.dma_start(part.rearrange("t p d -> p t d"), zeros[:].unsqueeze(1).to_broadcast(
                    [P, part.shape[0], D])).then_inc(S["rows_zeroed"], 16)
            in_pairs(sp, 2, R0, lambda i, parity: load_rows(i, parity, "early"))
            sp.wait_ge(S["scattered"], 16 * TOP * NT)
            in_pairs(sp, R0, R1, lambda i, parity: load_rows(i, parity, "routed"))
            sp.wait_ge(S["x2_out"], 16 * NT)
            in_pairs(sp, R1, TILES, lambda i, parity: load_rows(i, parity, "late"))

            def store_out(t, n):
                sp.dma_start(out_v[:, bass.ds(t, n), :], xres[:, bass.ds(t, n), :]).then_inc(S["out_stored"], 16)

            def store_pair(j):
                sp.wait_ge(S["out_ready"], 2 * j + 2)
                store_out(2 * j, 2)

            each(sp, 0, NT // 2 - 1, store_pair)
            sp.wait_ge(S["out_ready"], NT - 1)
            store_out(NT - 2, 1)
            sp.wait_ge(S["y_done"], NT)
            store_out(NT - 1, 1)
            sp.wait_ge(S["out_stored"], 16 * (NT // 2 + 1))
            sp.wait_ge(S["rows_zeroed"], 16 * NB)

        @block.gpsimd
        def _(pool):
            def load_w1(p, src):
                pool.dma_start(stage1[:], src).then_inc(S["stage1_in"], 16)

            def load_w2(p, src):
                pool.dma_start(stage2[:], src).then_inc(S["stage2_in"], 16)

            sW1_v, sW2_v = chunked(sW1), chunked(sW2)
            pool.memset(ident[:], 0.0).then_inc(S["consts"], 1)
            pool.memset(ones[:], 1.0).then_inc(S["consts"], 1)
            pool.memset(before[:], 1.0).then_inc(S["consts"], 1)
            pool.memset(headmask[:], 1.0).then_inc(S["consts"], 1)
            pool.memset(pairmask[:], 1.0).then_inc(S["consts"], 1)
            pool.memset(earlier[:], 1.0).then_inc(S["consts"], 1)
            pool.iota(iota_i[:], pattern=[[1, E]], base=0, channel_multiplier=0).then_inc(S["consts"], 1)
            pool.wait_ge(S["consts"], 7)
            pool.affine_select(out=ident[:], in_=ident[:], compare_op=ALU.not_equal, fill=1.0, base=0,
                               pattern=[[-1, P]], channel_multiplier=1).then_inc(S["consts"], 1)
            pool.affine_select(out=before[:], in_=before[:], compare_op=ALU.is_gt, fill=0.0, base=0,
                               pattern=[[1, P]], channel_multiplier=-1).then_inc(S["consts"], 1)
            pool.affine_select(out=headmask[:], in_=headmask[:], compare_op=ALU.is_ge, fill=0.0, base=0,
                               pattern=[[-DH, HC]], channel_multiplier=1).then_inc(S["consts"], 1)
            for j, (h0, h1, pair, _) in enumerate(CHUNKS):
                m = pairmask[:, pair:pair + h1 - h0]
                ge = pool.affine_select(out=m, in_=m, compare_op=ALU.is_ge, fill=0.0, base=j * P - h0 * SK,
                                        pattern=[[-SK, h1 - h0]], channel_multiplier=1)
            ge.then_inc(S["consts"], 1)
            pool.affine_select(out=earlier[:], in_=earlier[:], compare_op=ALU.is_gt, fill=0.0, base=0,
                               pattern=[[1, E], [-1, E]], channel_multiplier=0).then_inc(S["consts"], 1)
            pool.wait_ge(S["consts"], 12)
            pool.affine_select(out=headmask[:], in_=headmask[:], compare_op=ALU.is_ge, fill=0.0, base=DH - 1,
                               pattern=[[DH, HC]], channel_multiplier=-1).then_inc(S["consts"], 1)
            for j, (h0, h1, pair, _) in enumerate(CHUNKS):
                m = pairmask[:, pair:pair + h1 - h0]
                le = pool.affine_select(out=m, in_=m, compare_op=ALU.is_ge, fill=0.0, base=(h0 + 1) * SK - 1 - j * P,
                                        pattern=[[SK, h1 - h0]], channel_multiplier=-1)
            le.then_inc(S["consts"], 1)
            pool.dma_start(bv_bc[:], bv.partition_broadcast(P)).then_inc(S["bv_in"], 16)
            pool.dma_start(gate_r[:], gate_w).then_inc(S["gate_w_in"], 16)
            pool.dma_start(bo_bc[:], bo.partition_broadcast(P)).then_inc(S["bo_in"], 16)
            pool.wait_ge(S["consts"], 14)
            pool.wait_ge(S["x_in1"], 16)
            load_w1(0, sW1_v)
            load_w2(0, sW2_v)

            def key_diag(b):
                pool.wait_ge(S["kT_lo"], C if (b + 1) * SK <= CTX // 2 else 2 * C)
                if b >= 2:
                    pool.wait_ge(S["s_ps"], TB * (b - 1))
                for c in range(C):
                    for whole, part in ((kTh, kdh), (kTl, kdl)):
                        pool.tensor_tensor(
                            part[:, b % 2, c, :, :],
                            whole[:, c, b * SK:(b + 1) * SK].bitcast(F32).unsqueeze(1).to_broadcast([P, HC, SK]),
                            headmask[:].unsqueeze(2).to_broadcast([P, HC, SK]), ALU.mult
                        ).then_inc(S["kd_ready"], 1)

            def load_hi1(s, src):
                pool.dma_start(w1h[:, bass.ds(s, 1), :, :].rearrange("p o c f -> p (o c) f"), src
                               ).then_inc(S["w1h_in"], 16)

            def load_hi2(s, src):
                pool.dma_start(w2hl[:, bass.ds(s, 1), :, 0:D].rearrange("p o c f -> p (o c) f"), src
                               ).then_inc(S["w2h_in"], 16)

            def split_w1(p, s):
                pool.wait_ge(S["stage1_in"], 16 * p + 16)
                pool.wait_ge(S["w1h_in"], 16 * p + 16)
                hi = w1h[:, bass.ds(s, 1), :, :].rearrange("p o c f -> p (o c) f")
                lo = w1l[:, bass.ds(s, 1), :, :].rearrange("p o c f -> p (o c) f")
                pool.tensor_tensor(lo, stage1[:], hi.bitcast(F32), ALU.subtract).then_inc(S["split_w1"], 1)
                met(pool)
                pool.wait_ge(S["split_w1"], p + 1)

            def split_w2(p, s):
                pool.wait_ge(S["stage2_in"], 16 * p + 16)
                pool.wait_ge(S["w2h_in"], 16 * p + 16)
                both = w2hl[:, bass.ds(s, 1), :, :].rearrange("p o c f -> p (o c) f")
                pool.tensor_tensor(both[:, :, D:2 * D], stage2[:], both[:, :, 0:D].bitcast(F32),
                                   ALU.subtract).then_inc(S["split_w2"], 1)
                met(pool)
                pool.wait_ge(S["split_w2"], p + 1)

            def load_b1(s, src):
                pool.dma_start(b1bc[:, bass.ds(s, 1), :].rearrange("p o f -> p (o f)"), src).then_inc(S["b1_in"], 16)

            def load_b2(s, src):
                pool.dma_start(b2bc[:, bass.ds(s, 1), :].rearrange("p o f -> p (o f)"), src).then_inc(S["b2_in"], 16)

            def ready_1(p):
                met(pool)
                pool.wait_ge(S["b1_in"], 16 * p + 16)
                pool.sem_inc(S["w1_ready"], 1)

            def ready_2(p):
                pool.wait_ge(S["b2_in"], 16 * p + 16)
                pool.sem_inc(S["w2_ready"], 1)

            shared_b = (sb1.partition_broadcast(P), sb2.partition_broadcast(P))
            expert_b = lambda e: (b1[bass.ds(e, 1), :].rearrange("o f -> (o f)").partition_broadcast(P),
                                  b2[bass.ds(e, 1), :].rearrange("o f -> (o f)").partition_broadcast(P))
            expert_w1 = lambda e: W1_v[bass.ds(e, 1)].rearrange("o p c f -> p (o c) f")
            expert_w2 = lambda e: W2_v[bass.ds(e, 1)].rearrange("o p c f -> p (o c) f")

            pool.wait_ge(S["zero_set"], 1)
            key_diag(0)
            load_b1(0, shared_b[0])
            load_b2(0, shared_b[1])
            load_hi1(0, sW1_v)
            load_hi2(0, sW2_v)
            key_diag(1)
            split_w1(0, 0)
            load_w1(1, expert_w1(0))
            ready_1(0)
            key_diag(2)
            split_w2(0, 0)
            load_w2(1, expert_w2(0))
            ready_2(0)
            load_b1(1, expert_b(0)[0])
            load_b2(1, expert_b(0)[1])
            load_hi1(1, expert_w1(0))
            load_hi2(1, expert_w2(0))
            key_diag(3)
            split_w1(1, 1)
            load_w1(2, expert_w1(1))
            ready_1(1)
            key_diag(4)
            split_w2(1, 1)
            load_w2(2, expert_w2(1))
            ready_2(1)
            for b in range(5, B):
                key_diag(b)
            pool.wait_ge(S["l_sb"], NT)
            pool.iota(tile_i[:], pattern=[[1, TILES], [0, PH - 1]], base=0, channel_multiplier=0).then_inc(S["tiles_set"], 1)

            pool.wait_ge(S["slots_set"], 1)
            pool.wait_ge(S["rows_zeroed"], 16 * NB)
            pool.wait_ge(S["x2_out"], 16 * NT)
            for t in range(NT):
                for k in range(TOP):
                    pool.indirect_dma_start(
                        out=rows, out_offset=bass.IndirectOffsetOnAxis(ap=slot[:, k, t:t + 1], axis=0),
                        in_=x2[:, t, :], in_offset=None).then_inc(S["scattered"], 16)

            def phase(p, s, bias, here, ahead):
                first = pool.value_load(first_tile[0:1, bass.ds(p - 1, 1)], min_val=R0, max_val=R1)
                halves = pool.value_load(first_half[0:1, bass.ds(p - 1, 1)], min_val=2 * R0, max_val=2 * R1)
                met(pool)
                pool.wait_ge(S["h_add"], halves)
                load_hi1(s, here[0])
                load_b1(s, bias[0])
                split_w1(p, s)
                if ahead:
                    load_w1(p + 1, ahead[0])
                ready_1(p)
                met(pool)
                pool.wait_ge(S["y_sum"], first)
                load_hi2(s, here[1])
                load_b2(s, bias[1])
                split_w2(p, s)
                if ahead:
                    load_w2(p + 1, ahead[1])
                ready_2(p)

            pool.wait_ge(S["tables_set"], 1)
            with pool.Fori(2, E) as p:
                phase(p, p % 2, expert_b(p - 1), (expert_w1(p - 1), expert_w2(p - 1)), (expert_w1(p), expert_w2(p)))
            phase(E, E % 2, expert_b(E - 1), (expert_w1(E - 1), expert_w2(E - 1)), (sW1_v, sW2_v))
            phase(E + 1, (E + 1) % 2, shared_b, (sW1_v, sW2_v), None)

            pool.wait_ge(S["y_stored"], 16 * NR)
            for t in range(NT):
                for k in range(TOP):
                    pool.indirect_dma_start(
                        out=gath[:, t, k, :], out_offset=None, in_=routed_y,
                        in_offset=bass.IndirectOffsetOnAxis(ap=slot[:, k, t:t + 1], axis=0)
                    ).then_inc(g_in[t // 2], 16)

        @block.tensor
        def _(pe):
            mm = nc.tensor.matmul
            pe.wait_ge(S["consts"], 8)
            pe.wait_ge(S["ctx_in"], 32)
            for k in range(NCT):
                n = min(P, CTX - k * P)
                dst = ps[:, k, :]
                for c in range(C):
                    last = nc.tensor.transpose(dst[:, c * P:c * P + n], ctx_r[0:n, k, c * P:(c + 1) * P],
                                               ident[0:n, 0:n])
                last.then_inc(S["ctxT_ps"], 1)
            pe.wait_ge(S["wk_in"], 16)
            pe.wait_ge(S["ctxT_sb"], NCT)
            HALF = CTX // 2
            for n in range(2):
                for co in range(C):
                    for ci in range(C):
                        last = mm(ps[:, k_banks[C * n + co], 0:HALF], wk[:, ci, co * P:(co + 1) * P],
                                  ctxT[:, ci, n * HALF:(n + 1) * HALF], start=ci == 0, stop=ci == C - 1)
                    last.then_inc(S["kT_ps"], 1)
            def values(batches):
                for b in batches:
                    dst = ps[0:SK, v_banks[b // 2], :]
                    for ci in range(C):
                        last = mm(dst[:, (b % 2) * D:(b % 2 + 1) * D], ctxT[:, ci, b * SK:(b + 1) * SK], wv[:, ci, :],
                                  start=ci == 0, stop=ci == C - 1)
                    if b % 2:
                        last.then_inc(S["v_ps"], 1)

            def turn_gate():
                for c in range(C):
                    last = nc.tensor.transpose(p_in[:, c * E:(c + 1) * E], gate_r[:, c * P:(c + 1) * P],
                                               ident[0:E, 0:E])
                last.then_inc(S["gT_ps"], 1)

            def turn_rows(i, parity):
                pe.wait_ge(xrow_in[parity], 8 * (i - parity) + 16)
                for c in range(C):
                    last = nc.tensor.transpose(p_x[:, c, :], xrow[:, parity, c * P:(c + 1) * P], ident[:])
                last.then_inc(S["xT_ps"], 1)

            def turn_hidden(i):
                for n in range(2):
                    pe.wait_ge(S["h_act"], 2 * i + n + 1)
                    for c in range(FC // 2):
                        last = nc.tensor.transpose(p_hT[:, n, c, :], hid[:, n, c * P:(c + 1) * P], ident[:])
                    last.then_inc(S["hT_ps"], 1)

            def up(i, p, s):
                pe.wait_ge(S["w1_ready"], p + 1)
                pe.wait_ge(S["xT_lo"], i + 1)
                for n in range(2):
                    if not isinstance(i, int) or i >= 1:
                        pe.wait_ge(S["h_add"], 2 * i - 1 + n)
                    part = lambda w, c: w[:, bass.ds(s, 1), c, n * (F // 2):(n + 1) * (F // 2)].rearrange(
                        "p o f -> p (o f)")
                    for c in range(C):
                        mm(p_h[:, n, :], xTh[:, c, :], part(w1l, c), start=c == 0, stop=False)
                        mm(p_h[:, n, :], xTh[:, c, :], part(w1h, c), start=False, stop=False)
                        last = mm(p_h[:, n, :], xTl[:, c, :], part(w1h, c), start=False, stop=c == C - 1)
                    last.then_inc(S["h_ps"], 1)

            def down(i, p, s):
                pe.wait_ge(S["w2_ready"], p + 1)
                if not isinstance(i, int) or i >= 1:
                    pe.wait_ge(S["y_sum"], i)
                for c in range(FC):
                    if c % (FC // 2) == 0:
                        pe.wait_ge(S["hT_lo"], 2 * i + 1 + c // (FC // 2))
                    part = lambda n: w2hl[:, bass.ds(s, 1), c, 0:n].rearrange("p o f -> p (o f)")
                    mm(p_y, hTh[:, c, :], part(2 * D), start=c == 0, stop=False)
                    last = mm(p_y[:, 0:D], hTl[:, c, :], part(D), start=False, stop=c == FC - 1)
                last.then_inc(S["y_ps"], 1)

            def norm_in(t, bank=p_wo):
                pe.wait_ge(S["xn_ready"], t + 1)
                for c in range(C):
                    last = nc.tensor.transpose(bank[:, c * P:(c + 1) * P], xn[:, c * P:(c + 1) * P], ident[:])
                last.then_inc(S["xnT_ps"], 1)

            def queries(t):
                pe.wait_ge(S["xnT_sb"], t + 1)
                for co in range(C):
                    for ci in range(C):
                        last = mm(p_in[:, co * P:(co + 1) * P], wq[:, ci, co * P:(co + 1) * P], xnT[:, ci, :],
                                  start=ci == 0, stop=ci == C - 1)
                last.then_inc(S["q_ps"], 1)

            def scores(t):
                if not isinstance(t, int) or t >= 1:
                    pe.wait_ge(S["p_sub"], t)
                pe.wait_ge(S["q_sb"], t + 1)
                b = t // TB
                pe.wait_ge(S["kd_ready"], 2 * C * (b + 1))
                for c, h0, h1, n, col in score_parts:
                    dst = ps[:, n, col:col + (h1 - h0) * SK]
                    for q, keys in ((qTh, kdl), (qTh, kdh), (qTl, kdh)):
                        mm(dst, q[:, c, :], keys[:, bass.ds(b % 2, 1), c, h0:h1, :].rearrange("p o h k -> p (o h k)"),
                           start=keys is kdl, stop=False)
                    masked = mask_bf[0:1, bass.ds(b * SK, SK)].unsqueeze(1).to_broadcast([1, h1 - h0, SK])
                    last = mm(dst, ones_bf[0:1, :], masked, start=False, stop=True)
                last.then_inc(S["s_ps"], 1)

            def spread(q):
                pair, (j0, j1) = q // 2, SPREAD[q % 2]
                first = CHUNKS[j0][2]
                wide = CHUNKS[j1 - 1][2] + CHUNKS[j1 - 1][1] - CHUNKS[j1 - 1][0] - first
                out_v = ps[:, spread_bank[q], 0:2 * wide * (DH + 1)].rearrange("p (b n d) -> p b n d", b=2, d=DH + 1)
                for j in range(j0, j1):
                    h0, h1, at, n = CHUNKS[j]
                    key0 = j * P % SK
                    last = mm(out_v[0:n, :, at - first:at - first + h1 - h0, :],
                              copies[:].rearrange("k o q -> k (o q)")[:, key0:key0 + n],
                              vals[:, 2 * pair:2 * pair + 2, h0:h1, :], start=True, stop=True)
                last.then_inc(S["v_spread_ps"], 1)

            def turn_probs(t, g):
                if g == 0:
                    pe.wait_ge(S["p_exp"], t + 1)
                    if not isinstance(t, int) or t >= 1:
                        pe.wait_ge(S["pt_sb"], 3 * t)
                if g == 2:
                    pe.wait_ge(S["pt_sb"], 3 * t + 1)
                j0, j1 = PARTS[g]
                for j in range(j0, j1):
                    n = CHUNKS[j][3]
                    last = nc.tensor.transpose(ps[0:n, part_bank[g], (j - j0) * P:(j - j0 + 1) * P],
                                               front[:, j * P:j * P + n], ident[:])
                last.then_inc(S["pt_ps"], 1)

            def attend(t, j0, j1):
                if j0 == 0:
                    if not isinstance(t, int) or t >= 1:
                        pe.wait_ge(S["o_norm"], t)
                    mm(p_o, zeros_bf[:, 0:P], zeros_bf[:].rearrange("o (h d) -> o h d", d=DH + 1),
                       start=True, stop=False)
                g = [n for n, (a0, a1) in enumerate(PARTS) if a0 < j1 <= a1][0]
                pe.wait_ge(S["pt_sb"], 3 * t + g + 1)
                for j in range(j0, j1):
                    h0, h1, at, n = CHUNKS[j]
                    last = mm(p_o[:, h0:h1, :], probT[0:n, j, :],
                              spread_v[0:n, bass.ds(t // TB, 1), at:at + h1 - h0, :].rearrange("k o n d -> k (o n) d"),
                              start=False, stop=j == NCH - 1)
                if j1 == PARTS[g][1]:
                    last.then_inc(S["pv_part"], 1)

            def turn_heads(t):
                pe.wait_ge(S["o_norm"], t + 1)
                if not isinstance(t, int) or t >= 1:
                    pe.wait_ge(S["x1_mid"], t)
                for c in range(C):
                    last = nc.tensor.transpose(p_wo[:, c * P:(c + 1) * P], o_n[:, c * P:(c + 1) * P], ident[:])
                last.then_inc(S["oT_ps"], 1)

            def project(t):
                pe.wait_ge(S["oT_sb"], t + 1)
                for c in range(C):
                    last = mm(p_wo, oT[:, c, :], wo[:, c, :], start=c == 0, stop=c == C - 1)
                last.then_inc(S["wo_ps"], 1)

            def turn_x2(t):
                pe.wait_ge(S["x2_ready"], t + 1)
                for c in range(C):
                    last = nc.tensor.transpose(p_in[:, c * P:(c + 1) * P], x2row[:, c * P:(c + 1) * P], ident[:])
                last.then_inc(S["x2T_ps"], 1)

            def route_logits(t):
                pe.wait_ge(S["x2T_sb"], t + 1)
                for c in range(C):
                    last = mm(p_l, x2T[:, c, :], gateT[:, c, :], start=c == 0, stop=c == C - 1)
                last.then_inc(S["l_ps"], 1)

            def step(t):
                known = isinstance(t, int)
                ok = lambda u: not known or 0 <= u < NT
                if ok(t - 3):
                    pe.wait_ge(S["q_sb"], t + 2 if ok(t + 1) else NT)
                    route_logits(t - 3)
                if known and t == 0:
                    pe.wait_ge(S["gate_w_in"], 16)
                    pe.wait_ge(S["q_sb"], 2)
                    turn_gate()
                    pe.wait_ge(S["v_spread"], 2)
                    spread(4)
                    spread(5)
                if known and t == 1:
                    spread(6)
                if known and t == 2:
                    pe.wait_ge(S["x1_mid"], 1)
                    spread(7)
                if ok(t + 1):
                    scores(t + 1)
                if ok(t + 2):
                    if ok(t - 2):
                        pe.wait_ge(S["x1_mid"], t - 1)
                    if known and t in (0, 1, 2):
                        pe.wait_ge(S["v_spread"], (5, 7, 8)[t])
                    norm_in(t + 2)
                if known and t in (0, 1, 2):
                    pe.wait_ge(S["v_spread"], (6, 7, 8)[t])
                if known and t == NT - 1:
                    pe.wait_ge(S["l_sb"], t - 2)
                    turn_rows(0, 0)
                if ok(t):
                    turn_probs(t, 0)
                    turn_probs(t, 1)
                if ok(t - 1):
                    pe.wait_ge(S["xnT_sb"], t + 3 if ok(t + 2) else NT)
                    turn_heads(t - 1)
                if ok(t - 2):
                    if ok(t - 3):
                        pe.wait_ge(S["l_sb"], t - 2)
                    if known and t == NT - 1:
                        pe.wait_ge(S["xT_lo"], 1)
                    turn_x2(t - 2)
                if ok(t):
                    turn_probs(t, 2)
                    attend(t, 0, 4)
                if ok(t + 2):
                    if ok(t - 2):
                        pe.wait_ge(S["x2T_sb"], t - 1)
                    if known and t == 0:
                        pe.wait_ge(S["gT_sb"], 1)
                    queries(t + 2)
                if ok(t - 1):
                    project(t - 1)
                if ok(t):
                    attend(t, 4, 8)
                    attend(t, 8, NCH)
                if known and t == NT - 1:
                    up(0, 0, 0)

            pe.wait_ge(S["wv_in"], 16)
            values((0, 1))
            norm_in(0, p_in)
            pe.wait_ge(S["wq_in"], 16)
            queries(0)
            pe.wait_ge(S["kT_lo"], 2 * C)
            values(range(2, B))
            pe.wait_ge(S["q_sb"], 1)
            norm_in(1, p_in)
            pe.wait_ge(S["mask_set"], 2)
            scores(0)
            queries(1)
            pe.wait_ge(S["v_sb"], B // 2)
            pe.wait_ge(S["copies_set"], 1)
            for q in range(4):
                spread(q)
            pe.wait_ge(S["wo_in"], 16)
            step(0)
            step(1)
            step(2)
            each(pe, 3, NT - 2, step)
            for t in range(NT - 2, NT + 3):
                step(t)

            def places():
                pe.wait_ge(S["chosen_set"], 1)
                mm(p_place, before[:], chosen[:], start=True, stop=False)
                for u in range(NT):
                    last = mm(p_place[:, u + 1:NT + 1, :], ones[:],
                              chosen[:, u:u + 1, :].to_broadcast([P, NT - u, E]), start=False, stop=u == NT - 1)
                last.then_inc(S["rank_ps"], 1)

            def phase_at(i):
                if isinstance(i, int) and i < R0:
                    return 0, 0
                if isinstance(i, int) and i >= R1:
                    return PH - 1, (PH - 1) % 2
                p = pe.value_load(phase_of[0:1, bass.ds(i, 1)], min_val=0, max_val=PH - 1)
                return p, p % 2

            def tile(i, parity, now=None, last=None, between=None):
                known = isinstance(i, int)
                turn_hidden(i - 1)
                if not known or i < TILES:
                    up(i, *(now or phase_at(i)))
                if between:
                    between()
                if not known or i < TILES - 1:
                    turn_rows(i + 1, 1 - parity)
                down(i - 1, *(last or phase_at(i - 1)))

            pe.wait_ge(S["l_sb"], NT)
            turn_rows(1, 1)
            tile(1, 1, (0, 0), (0, 0), places)
            in_pairs(pe, 2, R0, lambda i, parity: tile(i, parity, (0, 0), (0, 0)))
            pe.wait_ge(S["tables_set"], 2)
            tile(R0, R0 % 2)
            in_pairs(pe, R0 + 1, TILES - 1, tile)
            tile(TILES - 1, (TILES - 1) % 2)
            tile(TILES, TILES % 2)

        @block.scalar
        def _(act):
            act.dma_start(gates[:, 0:1], g_xattn.partition_broadcast(P)).then_inc(S["gates_in"], 16)
            act.dma_start(gates[:, 1:2], g_ffn.partition_broadcast(P)).then_inc(S["gates_in"], 16)
            by_chunk = lambda v: v.rearrange("(c p) -> p c", p=P)
            act.dma_start(bkT[:], by_chunk(bk), allow_slow_non_contiguous=True).then_inc(S["bk_in"], 16)
            act.wait_ge(S["gates_in"], 32)
            act.activation(tgate[:], gates[:], ACT.Tanh).then_inc(S["gate_tanh"], 1)
            act.preload_act_table_set("natural_log_exp_and_others")
            act.dma_start(mask_u8[:], mask.rearrange("b k -> (b k)").unsqueeze(0)).then_inc(S["mask_in"], 16)
            act.dma_start(bqT[:], by_chunk(bq), allow_slow_non_contiguous=True).then_inc(S["bq_in"], 16)
            act.wait_ge(S["bk_in"], 16)

            def keys_hi(m):
                act.wait_ge(S["kT_ps"], m + 1)
                n, co = m // C, m % C
                act.activation(kTh[:, co, n * CTX // 2:(n + 1) * CTX // 2], ps[:, k_banks[m], 0:CTX // 2],
                               ACT.Identity, bias=bkT[:, co:co + 1]).then_inc(S["kT_sb"], 1)

            def deviations(part, t0, t1):
                act.wait_ge(S["ln_mv"], t1)
                act.activation(lnv[:, t0:t1], mv[:, t0:t1, 1], ACT.Ln, bias=eps[:, 0:1]).then_inc(S["ln_log"], 1)
                act.wait_ge(S["ln_log"], part + 1)
                act.activation(rstd[:, t0:t1], lnv[:, t0:t1], ACT.Exp, scale=-0.5).then_inc(S["ln_rstd"], 1)

            def norm_in(t, bank=p_wo):
                act.wait_ge(S["xnT_ps"], t + 1)
                act.activation(xnT[:].rearrange("p c q -> p (c q)"), bank, ACT.Copy).then_inc(S["xnT_sb"], 1)

            def queries(t):
                act.wait_ge(S["q_ps"], t + 1)
                if not isinstance(t, int) or t >= 1:
                    act.wait_ge(S["s_ps"], t)
                for c in range(C):
                    last = act.activation(qTh[:, c, :], p_in[:, c * P:(c + 1) * P], ACT.Identity, bias=bqT[:, c:c + 1])
                last.then_inc(S["q_hi"], 1)

            def exponent(t):
                act.wait_ge(S["p_sub"], t + 1)
                act.activation(front[:, 0:H * SK], front[:, 0:H * SK], ACT.Exp, scale=SCALE).then_inc(S["p_exp"], 1)

            def turned_probs(t, g):
                act.wait_ge(S["pt_ps"], 3 * t + g + 1)
                if not isinstance(t, int) or t >= 1:
                    act.wait_ge(S["pv_part"], 3 * t + g - 2)
                j0, j1 = PARTS[g]
                act.activation(probT[:, j0:j1, :], ps[:, part_bank[g], 0:(j1 - j0) * P].rearrange(
                    "p (j q) -> p j q", q=P), ACT.Copy).then_inc(S["pt_sb"], 1)

            def turned_heads(t):
                act.wait_ge(S["oT_ps"], t + 1)
                act.activation(oT[:].rearrange("p c q -> p (c q)"), p_wo, ACT.Copy).then_inc(S["oT_sb"], 1)

            def rows_hi(i):
                act.wait_ge(S["xT_ps"], i + 1)
                act.activation(xTh[:], p_x, ACT.Copy).then_inc(S["xT_hi"], 1)

            def turned_x2(t):
                act.wait_ge(S["x2T_ps"], t + 1)
                if not isinstance(t, int) or t >= 1:
                    act.wait_ge(S["l_ps"], t)
                act.activation(x2T[:].rearrange("p c q -> p (c q)"), p_in, ACT.Copy).then_inc(S["x2T_sb"], 1)

            def deviation(t):
                act.wait_ge(S["mv2_done"], t + 1)
                act.activation(lnv2[:], mv2[:, 1:2], ACT.Ln, bias=eps[:, 0:1]).then_inc(S["ln2_log"], 1)
                act.activation(nw2[:, 0:1], mv2[:, 1:2], ACT.Identity, bias=neg_eps[:, 0:1], scale=-0.5
                               ).then_inc(S["nw_a"], 1)
                act.wait_ge(S["ln2_log"], t + 1)
                act.activation(r2[:], lnv2[:], ACT.Exp, scale=-0.5).then_inc(S["r2_done"], 1)
                act.wait_ge(S["r2_done"], t + 1)
                act.activation(nw2[:, 1:2], r2[:], ACT.Square).then_inc(S["nw_b"], 1)
                act.wait_ge(S["nw_b"], t + 1)
                act.wait_ge(S["nw_a"], t + 1)
                act.activation(nw2[:, 2:3], nw2[:, 1:2], ACT.Identity, scale=nw2[:, 0:1], bias=one_half[:, 0:1]
                               ).then_inc(S["nw_c"], 1)
                act.wait_ge(S["nw_c"], t + 1)
                act.activation(nw2[:, 3:4], nw2[:, 2:3], ACT.Copy, scale=r2[:, 0:1]).then_inc(S["nw_d"], 1)

            def step(t):
                ok = lambda u: not isinstance(t, int) or 0 <= u < NT
                if ok(t + 2):
                    norm_in(t + 2)
                if isinstance(t, int) and t == NT - 1:
                    rows_hi(0)
                if ok(t):
                    turned_probs(t, 0)
                    turned_probs(t, 1)
                if ok(t - 1):
                    turned_heads(t - 1)
                if ok(t - 2):
                    turned_x2(t - 2)
                if ok(t):
                    turned_probs(t, 2)
                if ok(t + 2):
                    queries(t + 2)
                if ok(t + 1):
                    exponent(t + 1)
                if ok(t - 1):
                    deviation(t - 1)

            for m in range(C):
                keys_hi(m)
            deviations(0, 0, FIRST)
            for m in range(C, 2 * C):
                keys_hi(m)
            norm_in(0, p_in)
            act.wait_ge(S["bq_in"], 16)
            queries(0)
            norm_in(1, p_in)
            deviations(1, FIRST, NT)
            queries(1)
            exponent(0)
            step(0)
            step(1)
            each(act, 2, NT - 2, step)
            for t in range(NT - 2, NT + 2):
                step(t)

            def hidden_hi(i):
                for n in range(2):
                    act.wait_ge(S["hT_ps"], 2 * i + n + 1)
                    act.activation(hTh[:, n * (FC // 2):(n + 1) * (FC // 2), :], p_hT[:, n, :, :],
                                   ACT.Copy).then_inc(S["hT_hi"], 1)

            def gelu(i):
                for n in range(2):
                    act.wait_ge(S["h_add"], 2 * i + n + 1)
                    act.activation(hid[:, n, :], hid[:, n, :], ACT.Gelu).then_inc(S["h_act"], 1)

            def store_y(i):
                act.wait_ge(S["y_sum"], i + 1)
                act.dma_start(y_v[bass.ds(i - R0, 1)].rearrange("o p d -> (o p) d"), yrow[:]).then_inc(S["y_stored"], 16)

            def tile(i, store=False):
                known = isinstance(i, int)
                if not known or i >= 1:
                    hidden_hi(i - 1)
                if store:
                    store_y(i - 2)
                if not known or i < TILES:
                    gelu(i)
                if not known or i < TILES - 1:
                    rows_hi(i + 1)

            tile(0)
            tile(1)
            act.wait_ge(S["share_in"], 1)
            act.activation(lead[:, 1, :], lead[:, 0, :], ACT.Tanh, scale=0.5).then_inc(S["share_tanh"], 1)
            each(act, 2, R0 + 2, tile)
            each(act, R0 + 2, R1 + 2, lambda i: tile(i, True))
            each(act, R1 + 2, TILES - 1, tile)
            tile(TILES - 1)
            tile(TILES)

        @block.vector
        def _(dve):
            tt, ts, stt = dve.tensor_tensor, dve.tensor_scalar, dve.scalar_tensor_tensor
            dve.memset(zeros[:], 0.0).then_inc(S["zero_set"], 1)
            dve.memset(eps[:], EPS)
            dve.memset(neg_eps[:], -0.5 * EPS)
            dve.memset(one_half[:], 1.5)
            dve.memset(vals[:], 1.0).then_inc(S["mask_set"], 1)
            dve.memset(ones_bf[:], 1.0)
            dve.memset(zeros_bf[:], 0.0)
            dve.wait_ge(S["consts"], 8)
            ts(iota_far[:], iota_i[:], -FAR, None, ALU.add).then_inc(S["far_set"], 1)
            dve.tensor_copy(copies[:], ident[0:SK, 0:SK].unsqueeze(1).to_broadcast([SK, 3, SK])
                            ).then_inc(S["copies_set"], 1)
            for k in range(NCT):
                n = min(P, CTX - k * P)
                dve.wait_ge(S["ctxT_ps"], k + 1)
                dve.tensor_copy(ctxT[:, :, k * P:k * P + n],
                                ps[:, k, 0:C * P].rearrange("p (c q) -> p c q", q=P)[:, :, 0:n]
                                ).then_inc(S["ctxT_sb"], 1)

            def statistics(t0, t1):
                for t in range(t0, t1):
                    dve.bn_stats(stats[:, t, :], xres[:, t, :]).then_inc(S["ln_stats"], 1)

            def moments(t0, t1):
                for t in range(t0, t1):
                    dve.wait_ge(S["ln_stats"], t + 1)
                    dve.bn_aggr(mv[:, t, :], stats[:, t, :]).then_inc(S["ln_mv"], 1)

            def keys_lo(m):
                dve.wait_ge(S["kT_sb"], m + 1)
                n, co = m // C, m % C
                part = slice(n * CTX // 2, (n + 1) * CTX // 2)
                stt(kTl[:, co, part], ps[:, k_banks[m], 0:CTX // 2], bkT[:, co:co + 1],
                    kTh[:, co, part].bitcast(F32), ALU.add, ALU.subtract).then_inc(S["kT_lo"], 1)

            def values(n):
                src = ps[0:SK, v_banks[n], :]
                dve.wait_ge(S["v_ps"], n + 1)
                tt(vals[:, 2 * n:2 * n + 2, :, 0:DH],
                   src.rearrange("k (b h d) -> k b h d", b=2, d=DH),
                   bv_bc[0:SK, :].rearrange("k (h d) -> k h d", d=DH).unsqueeze(1).to_broadcast([SK, 2, H, DH]),
                   ALU.add).then_inc(S["v_sb"], 1)

            def newton(part, t0, t1):
                dve.wait_ge(S["ln_rstd"], part + 1)
                n = 4 * part
                tt(nw[:, 0, t0:t1], rstd[:, t0:t1], rstd[:, t0:t1], ALU.mult).then_inc(S["ln_newton"], 1)
                dve.wait_ge(S["ln_newton"], n + 1)
                stt(nw[:, 1, t0:t1], mv[:, t0:t1, 1], EPS, nw[:, 0, t0:t1], ALU.add, ALU.mult
                    ).then_inc(S["ln_newton"], 1)
                dve.wait_ge(S["ln_newton"], n + 2)
                ts(nw[:, 2, t0:t1], nw[:, 1, t0:t1], -0.5, 1.5, ALU.mult, ALU.add).then_inc(S["ln_newton"], 1)
                dve.wait_ge(S["ln_newton"], n + 3)
                tt(rstd[:, t0:t1], rstd[:, t0:t1], nw[:, 2, t0:t1], ALU.mult).then_inc(S["ln_newton"], 1)
                dve.wait_ge(S["ln_newton"], n + 4)

            def col(ap, t):
                return ap[:, bass.ds(t, 1)]

            def row(ap, t):
                return ap[:, bass.ds(t, 1), :].rearrange("p o d -> p (o d)")

            def norm_in(t):
                if not isinstance(t, int) or t >= 1:
                    dve.wait_ge(S["xnT_ps"], t)
                ts(xn[:], row(xres, t), row(mv, t)[:, 0:1], col(rstd, t), ALU.subtract, ALU.mult
                   ).then_inc(S["xn_ready"], 1)

            def queries_lo(t):
                dve.wait_ge(S["q_hi"], t + 1)
                for c in range(C):
                    last = stt(qTl[:, c, :], p_in[:, c * P:(c + 1) * P], bqT[:, c:c + 1], qTh[:, c, :].bitcast(F32),
                               ALU.add, ALU.subtract)
                last.then_inc(S["q_sb"], 1)

            def score_max(t):
                dve.wait_ge(S["s_ps"], t + 1)
                dve.tensor_reduce(smax[:, 0:H12].rearrange("p (n h) -> p n h", n=2), p_s12, AX_X, ALU.max)
                dve.tensor_reduce(smax[:, H12:H], p_s3, AX_X, ALU.max).then_inc(S["s_max"], 1)

            def score_sub(t):
                if not isinstance(t, int) or t >= 1:
                    dve.wait_ge(S["pt_ps"], 3 * t)
                dve.wait_ge(S["s_max"], t + 1)
                tt(prob[:, 0:H12, :].rearrange("p (n h) k -> p n h k", n=2), p_s12,
                   smax[:, 0:H12].rearrange("p (n h) -> p n h", n=2).unsqueeze(3).to_broadcast([P, 2, HG[0], SK]),
                   ALU.subtract)
                tt(prob[:, H12:H, :], p_s3, smax[:, H12:H].unsqueeze(2).to_broadcast([P, HG[2], SK]),
                   ALU.subtract).then_inc(S["p_sub"], 1)

            def normalise(t):
                dve.wait_ge(S["pv_part"], 3 * t + 3)
                dve.reciprocal(rsum[:], p_o[:, :, DH]).then_inc(S["o_sum"], 1)
                if not isinstance(t, int) or t >= 1:
                    dve.wait_ge(S["oT_ps"], t)
                dve.wait_ge(S["o_sum"], t + 1)
                tt(o_n[:].rearrange("p (h d) -> p h d", d=DH), p_o[:, :, 0:DH],
                   rsum[:].unsqueeze(2).to_broadcast([P, H, DH]), ALU.mult).then_inc(S["o_norm"], 1)

            def spread_out(q):
                dve.wait_ge(S["v_spread_ps"], q + 1)
                pair, (j0, j1) = q // 2, SPREAD[q % 2]
                first = CHUNKS[j0][2]
                wide = CHUNKS[j1 - 1][2] + CHUNKS[j1 - 1][1] - CHUNKS[j1 - 1][0] - first
                full = wide if CHUNKS[j1 - 1][3] == P else CHUNKS[j1 - 1][2] - first
                src = ps[:, spread_bank[q], 0:2 * wide * (DH + 1)].rearrange("p (b n d) -> p b n d", b=2, d=DH + 1)
                for n, a0, a1 in ((P, 0, full), (CHUNKS[-1][3], full, wide)):
                    if a0 < a1:
                        last = tt(spread_v[0:n, 2 * pair:2 * pair + 2, first + a0:first + a1, :], src[0:n, :, a0:a1, :],
                                  pairmask[0:n, first + a0:first + a1].unsqueeze(1).unsqueeze(3).to_broadcast(
                                      [n, 2, a1 - a0, DH + 1]), ALU.mult)
                last.then_inc(S["v_spread"], 1)

            def residual(t):
                dve.wait_ge(S["wo_ps"], t + 1)
                stt(row(xres, t), p_wo, tgate[:, 0:1], row(xres, t), ALU.mult, ALU.add).then_inc(S["x1_mid"], 1)
                dve.wait_ge(S["x1_mid"], t + 1)
                stt(row(xres, t), bo_bc[:], tgate[:, 0:1], row(xres, t), ALU.mult, ALU.add).then_inc(S["x1_done"], 1)
                met(dve)
                dve.wait_ge(S["x1_done"], t + 1)
                dve.bn_stats(st2[:], row(xres, t)).then_inc(S["st2_done"], 1)
                met(dve)
                dve.wait_ge(S["st2_done"], t + 1)
                dve.bn_aggr(mv2[:], st2[:]).then_inc(S["mv2_done"], 1)

            def rows_lo(i):
                dve.wait_ge(S["xT_hi"], i + 1)
                tt(xTl[:], p_x, xTh[:].bitcast(F32), ALU.subtract).then_inc(S["xT_lo"], 1)

            def hidden_lo(i):
                for n in range(2):
                    dve.wait_ge(S["hT_hi"], 2 * i + n + 1)
                    part = slice(n * (FC // 2), (n + 1) * (FC // 2))
                    tt(hTl[:, part, :], p_hT[:, n, :, :], hTh[:, part, :].bitcast(F32), ALU.subtract
                       ).then_inc(S["hT_lo"], 1)

            def add_b1(i, s):
                for n in range(2):
                    dve.wait_ge(S["h_ps"], 2 * i + n + 1)
                    tt(hid[:, n, :], p_h[:, n, :],
                       b1bc[:, bass.ds(s, 1), n * (F // 2):(n + 1) * (F // 2)].rearrange("p o f -> p (o f)"),
                       ALU.add).then_inc(S["h_add"], 1)

            def norm_two(t):
                dve.wait_ge(S["nw_d"], t + 1)
                if not isinstance(t, int) or t >= 1:
                    dve.wait_ge(S["x2_out"], 16 * t)
                    dve.wait_ge(S["x2T_ps"], t)
                ts(x2row[:], row(xres, t), mv2[:, 0:1], nw2[:, 3:4], ALU.subtract, ALU.mult).then_inc(S["x2_ready"], 1)

            def keep_logits(t):
                dve.wait_ge(S["l_ps"], t + 1)
                dve.tensor_copy(row(logits, t), p_l).then_inc(S["l_sb"], 1)

            def step(t):
                ok = lambda u: not isinstance(t, int) or 0 <= u < NT
                if ok(t - 2):
                    norm_two(t - 2)
                if ok(t - 3):
                    keep_logits(t - 3)
                if isinstance(t, int) and t == NT - 1:
                    rows_lo(0)
                if isinstance(t, int) and t == NT:
                    add_b1(0, 0)
                for q in {0: (4, 5), 1: (6,), 2: (7,)}.get(t, ()) if isinstance(t, int) else ():
                    spread_out(q)
                if ok(t + 1):
                    score_max(t + 1)
                if ok(t + 1):
                    score_sub(t + 1)
                if ok(t + 2):
                    queries_lo(t + 2)
                if ok(t - 1):
                    residual(t - 1)
                if ok(t + 3):
                    norm_in(t + 3)
                if ok(t):
                    normalise(t)

            dve.wait_ge(S["x_in0"], 16)
            statistics(0, FIRST)
            moments(0, FIRST)
            for m in range(C):
                keys_lo(m)
            newton(0, 0, FIRST)
            norm_in(0)
            for m in range(C, 2 * C):
                keys_lo(m)
            dve.wait_ge(S["mask_in"], 16)
            ts(mask_bf[:], mask_u8[:], MASKED, None, ALU.mult).then_inc(S["mask_set"], 1)
            dve.wait_ge(S["bv_in"], 16)
            dve.wait_ge(S["mask_set"], 1)
            values(0)
            queries_lo(0)
            norm_in(1)
            values(1)
            dve.wait_ge(S["x_in1"], 16)
            statistics(FIRST, NT // 2)
            values(2)
            statistics(NT // 2, NT)
            moments(FIRST, NT)
            values(3)
            score_max(0)
            queries_lo(1)
            score_sub(0)
            norm_in(2)
            newton(1, FIRST, NT)
            dve.wait_ge(S["gate_tanh"], 1)
            dve.wait_ge(S["bo_in"], 16)
            dve.wait_ge(S["consts"], 14)
            for q in range(4):
                spread_out(q)
            dve.wait_ge(S["gT_ps"], 1)
            dve.tensor_copy(gateT[:], p_in[:, 0:C * E].rearrange("p (c e) -> p c e", e=E)).then_inc(S["gT_sb"], 1)
            for t in range(3):
                step(t)
            each(dve, 3, NT - 3, step)
            for t in range(NT - 3, NT + 3):
                step(t)

            n_route = [0]

            def then(instruction):
                n_route[0] += 1
                instruction.then_inc(S["route"], 1)
                dve.wait_ge(S["route"], n_route[0])

            bc = lambda ap: ap.unsqueeze(2).to_broadcast([P, NT, E])
            far = iota_far[:].unsqueeze(1).to_broadcast([P, NT, E])
            dve.memset(chosen[:], 0.0)
            dve.wait_ge(S["l_sb"], NT)
            dve.wait_ge(S["far_set"], 1)
            for k in range(TOP):
                lg = (logits, lg2)[k]
                then(dve.tensor_reduce(top[:, k, :], lg[:], AX_X, ALU.max))
                then(tt(rt[:], lg[:], bc(top[:, k, :]), ALU.is_equal))
                then(tt(rt[:], rt[:], far, ALU.mult))
                then(dve.tensor_reduce(pick[:, k, :], rt[:], AX_X, ALU.min))
                then(tt(hot[:, k, :, :], far, bc(pick[:, k, :]), ALU.is_equal))
                if k == 0:
                    then(stt(lg2[:], hot[:, 0, :, :], -1e30, logits[:], ALU.mult, ALU.add))
                    rows_lo(1)
            tt(chosen[:, 0:NT, :], hot[:, 0, :, :], hot[:, 1, :, :], ALU.add).then_inc(S["chosen_set"], 1)
            tt(lead[:, 0, :], top[:, 0, :], top[:, 1, :], ALU.subtract).then_inc(S["share_in"], 1)

            def result(i, s, kind):
                dve.wait_ge(S["y_ps"], i + 1)
                tt(ysum[:], p_y[:, 0:D], row(b2bc, s), ALU.add).then_inc(S["y_mid"], 1)
                dve.wait_ge(S["y_mid"], i + 1)
                if kind == "routed":
                    if not isinstance(i, int) or i > R0:
                        dve.wait_ge(S["y_stored"], 16 * (i - R0))
                if kind == "late" and i == R1:
                    dve.wait_ge(S["y_stored"], 16 * NR)
                tt(yrow[:], p_y[:, D:2 * D], ysum[:], ALU.add).then_inc(S["y_sum"], 1)
                if kind != "routed":
                    t = i if kind == "early" else i - NR
                    dve.wait_ge(S["y_sum"], i + 1)
                    if isinstance(t, int) and t == NT - 1:
                        dve.wait_ge(S["out_ready"], NT)
                    stt(row(xres, t), yrow[:], tgate[:, 1:2], row(xres, t), ALU.mult, ALU.add
                        ).then_inc(S["y_done"], 1)

            def phase_at(i):
                if isinstance(i, int) and i < R0:
                    return 0
                if isinstance(i, int) and i >= R1:
                    return (PH - 1) % 2
                return dve.value_load(phase_of[0:1, bass.ds(i, 1)], min_val=0, max_val=PH - 1) % 2

            def combine(t):
                dve.wait_ge(g_in[t // 2], 16 * 2 * TOP)
                dve.wait_ge(S["y_done"], min(t + 1, NT - 1))
                for k in range(TOP):
                    if k == 1:
                        dve.wait_ge(S["g_mid"], t + 1)
                    stt(xres[:, t, :], gath[:, t, k, :], share[:, k, t:t + 1], xres[:, t, :], ALU.mult, ALU.add
                        ).then_inc(S["g_mid"] if k == 0 else S["out_ready"], 1)

            COMBINED = ((), (0, 1), (2, 3, 4), (5, 6, 7), (8, 9, 10), (11, 12), (13, 14, 15))
            assert len(COMBINED) == NB

            def tile(i, kind, now=None, last=None, combined=(), between=None):
                known = isinstance(i, int)
                hidden_lo(i - 1)
                if not known or i < TILES:
                    add_b1(i, phase_at(i) if now is None else now)
                for t in combined[1:]:
                    combine(t - 1)
                if between:
                    between()
                if not known or i < TILES - 1:
                    rows_lo(i + 1)
                for t in combined[-1:]:
                    combine(t)
                result(i - 1, phase_at(i - 1) if last is None else last, kind)

            def slots():
                dve.wait_ge(S["rank_ps"], 1)
                then(ts(cnt_i[:, 0, :], p_place[:, NT, :], float(P - 1), None, ALU.add))
                then(ts(cnt_i[:, 1, :], cnt_i[:, 0, :], 7, None, ALU.logical_shift_right))
                then(ts(etiles[:], cnt_i[:, 1, :], 1.0, None, ALU.max))
                then(tt(etri[:], earlier[:], etiles[:].unsqueeze(1).to_broadcast([P, E, E]), ALU.mult))
                then(dve.tensor_reduce(ebase[:], etri[:], AX_X, ALU.add))
                then(stt(place[:], ebase[:].unsqueeze(1).to_broadcast([P, NT, E]), float(P), p_place[:, 0:NT, :],
                         ALU.mult, ALU.add))
                then(tt(onplace[:], hot[:], place[:].unsqueeze(1).to_broadcast([P, TOP, NT, E]), ALU.mult))
                then(dve.tensor_reduce(posf[:], onplace[:], AX_X, ALU.add))
                dve.tensor_copy(slot[:], posf[:]).then_inc(S["slots_set"], 1)

            def tables():
                dve.wait_ge(S["tiles_set"], 1)
                then(dve.tensor_copy(tile_f[:], tile_i[:]))
                then(dve.memset(starts[:], 0.0))
                then(ts(starts[0:1, 1:1 + E], ebase[0:1, :], float(R0), None, ALU.add))
                then(dve.memset(starts[0:1, 1 + E:PH], float(R1)))
                then(ts(first_half[:], starts[:], 2.0, None, ALU.mult))
                dve.tensor_copy(first_tile[:], starts[:]).then_inc(S["tables_set"], 1)

            def tile_phases():
                then(tt(started[:], tile_f[:], starts[0:1, 1:PH].unsqueeze(1).to_broadcast([1, TILES, PH - 1]),
                        ALU.is_ge))
                then(dve.tensor_reduce(phase_f[:], started[:], AX_X, ALU.add))
                dve.tensor_copy(phase_of[:], phase_f[:]).then_inc(S["tables_set"], 1)

            def shares():
                dve.wait_ge(S["share_tanh"], 1)
                for k, sign in ((0, 0.5), (1, -0.5)):
                    then(ts(half[:, k, :], lead[:, 1, :], sign, 0.5, ALU.mult, ALU.add))
                    then(ts(share[:, k, :], half[:, k, :], tgate[:, 1:2], None, ALU.mult))

            tile(1, "early", 0, 0, between=slots)
            tile(2, "early", 0, 0, between=tables)
            tile(3, "early", 0, 0, between=tile_phases)
            tile(4, "early", 0, 0, between=shares)
            dve.wait_ge(S["tables_set"], 2)
            each(dve, 5, R0, lambda i: tile(i, "early", 0, 0))
            tile(R0, "early")
            tile(R0 + 1, "routed")
            each(dve, R0 + 2, R1 + 1, lambda i: tile(i, "routed"))
            for i in range(R1 + 1, TILES + 1):
                tile(i, "late", combined=COMBINED[i - R1 - 1])


_INS = ['x', 'ctx_1024', 'mask_BxS2_bf0', 'g_xattn', 'g_ffn', 'L0_xattn_Wq', 'L0_xattn_bq', 'L0_xattn_Wk',
        'L0_xattn_bk', 'L0_xattn_Wv', 'L0_xattn_bv', 'L0_xattn_Wo', 'L0_xattn_bo', 'L0_ffn_gate_w', 'L0_ffn_W1',
        'L0_ffn_b1', 'L0_ffn_W2', 'L0_ffn_b2', 'L0_ffn_sW1', 'L0_ffn_sb1', 'L0_ffn_sW2', 'L0_ffn_sb2']


def kernel(**inputs):
    import numpy as np
    import concourse.bacc as bacc
    from concourse import mybir as mb
    from concourse.bass_utils import run_bass_kernel_spmd

    nc = bacc.Bacc("TRN2", target_bir_lowering=False, num_devices=1)
    arrays, args = {}, []
    for name in _INS:
        a = np.ascontiguousarray(inputs[name])
        arrays[f"in_{name}"] = a
        args.append(nc.dram_tensor(f"in_{name}", a.shape, mb.dt.from_np(a.dtype), kind="ExternalInput").ap())
    shape = inputs["x"].shape
    args.append(nc.dram_tensor("out_0", shape, mb.dt.float32, kind="ExternalOutput").ap())
    gated_cross_attention_and_moe(nc, *args)
    r = run_bass_kernel_spmd(nc, [arrays], core_ids=[0])
    return r.results[0]["out_0"]
```
